# Optimizing a Trainium2 kernel written in Bass

```python
import numpy as np
import jax
import jax.numpy as jnp

def _softmax(x, axis=-1):
    return jax.nn.softmax(x, axis=axis)
def _gelu(x):
    return jax.nn.gelu(x, approximate=True)
def _silu(x):
    return jax.nn.silu(x)
def _sigmoid(x):
    return jax.nn.sigmoid(x)
def _layernorm(x, axis=-1, eps=1e-5):
    m = jnp.mean(x, axis=axis, keepdims=True)
    v = jnp.var(x, axis=axis, keepdims=True)
    return (x - m) / jnp.sqrt(v + eps)
def _scatter_add(tgt, idx, src, axis=0):
    return tgt.at[idx].add(src)
def _segment_sum(src, seg, n):
    return jax.ops.segment_sum(src, seg, n)

kernel_name = 'mk_conv_preact_d1_conv_nchw256_f8da57'

def setup_inputs(seed: int = 0):
    np.random.seed(seed)
    _w = jnp.asarray
    def _rec_inputs():
        import jax
        import jax.numpy as jnp
        _gk = jax.random.key(seed)
        x = 7.22e-05 + 1 * jax.random.normal(jax.random.fold_in(_gk, 1), (8, 256, 64, 64), jnp.float32)
        return x
    x = _rec_inputs()
    def _L0_conv_setup():
        import jax, jax.numpy as jnp
        import numpy as np
        H = 8
        DK = 64
        L = 64
        BN_EPS = 1e-05

        def calc_reindexing_tensor(l, Lr):
            x = jnp.arange(l)[:, None, None]
            i = jnp.arange(l)[None, :, None]
            r = jnp.arange(-(Lr - 1), Lr)[None, None, :]
            return ((i - x == r) & (jnp.abs(i - x) <= Lr)).astype(jnp.float32)
        key = jax.random.key(seed)
        ks = jax.random.split(key, 6)
        b, c, x, y = (8, 256, 64, 64)
        dim_hidden = H * DK
        return {'img': jax.random.normal(ks[0], (b, c, x, y), jnp.float32), 'w_qkv': jax.random.normal(ks[1], (dim_hidden * 3, c), jnp.float32) * 0.02, 'w_out': jax.random.normal(ks[2], (c, dim_hidden), jnp.float32) * 0.02, 'b_out': jnp.zeros((c,), jnp.float32), 'rel_rows': jax.random.normal(ks[3], (2 * L - 1, DK), jnp.float32), 'rel_columns': jax.random.normal(ks[4], (2 * L - 1, DK), jnp.float32), 'bn_gamma': jnp.ones((DK,), jnp.float32), 'bn_beta': jnp.zeros((DK,), jnp.float32)}
    _L0_conv_all = _L0_conv_setup()
    _L0_conv_in = {k: v for k, v in _L0_conv_all.items() if k in ('w_qkv', 'w_out', 'b_out', 'rel_rows', 'rel_columns', 'bn_gamma', 'bn_beta', )}
    del _L0_conv_all

    return {
        "x": x,
        "L0_conv_w_qkv": _L0_conv_in["w_qkv"],
        "L0_conv_w_out": _L0_conv_in["w_out"],
        "L0_conv_b_out": _L0_conv_in["b_out"],
        "L0_conv_rel_rows": _L0_conv_in["rel_rows"],
        "L0_conv_rel_columns": _L0_conv_in["rel_columns"],
        "L0_conv_bn_gamma": _L0_conv_in["bn_gamma"],
        "L0_conv_bn_beta": _L0_conv_in["bn_beta"],
    }

def reference(x, L0_conv_w_qkv, L0_conv_w_out, L0_conv_b_out, L0_conv_rel_rows, L0_conv_rel_columns, L0_conv_bn_gamma, L0_conv_bn_beta):
    import jax
    import jax.numpy as jnp
    def _L0_conv_ref(img, w_qkv, w_out, b_out, rel_rows, rel_columns, bn_gamma, bn_beta):
        import jax, jax.numpy as jnp
        import numpy as np
        H = 8
        DK = 64
        L = 64
        BN_EPS = 1e-05

        def calc_reindexing_tensor(l, Lr):
            x = jnp.arange(l)[:, None, None]
            i = jnp.arange(l)[None, :, None]
            r = jnp.arange(-(Lr - 1), Lr)[None, None, :]
            return ((i - x == r) & (jnp.abs(i - x) <= Lr)).astype(jnp.float32)
        b, c, x, y = img.shape
        m = x * y
        qkv = jnp.einsum('bcxy,oc->boxy', img, w_qkv)
        q, k, v = jnp.split(qkv, 3, axis=1)
        q = q.reshape(b * H, DK, m)
        k = k.reshape(b * H, DK, m)
        v = v.reshape(b * H, DK, m)
        k = jax.nn.softmax(k, axis=-1)
        context = jnp.einsum('ndm,nem->nde', k, v)
        content_out = jnp.einsum('nde,ndm->nem', context, q)
        content_out = content_out.reshape(b * H, DK, x, y)
        q4 = q.reshape(b * H, DK, x, y)
        v4 = v.reshape(b * H, DK, x, y)
        Ix = calc_reindexing_tensor(x, L)
        Px = jnp.einsum('xir,rd->xid', Ix, rel_rows)
        Sx = jnp.einsum('ndxy,xid->nixy', q4, Px)
        Yh = jnp.einsum('nixy,neiy->nexy', Sx, v4)
        mean = Yh.mean(axis=(0, 2, 3), keepdims=True)
        var = Yh.var(axis=(0, 2, 3), keepdims=True)
        Yh = (Yh - mean) * jax.lax.rsqrt(var + BN_EPS)
        Yh = Yh * bn_gamma[None, :, None, None] + bn_beta[None, :, None, None]
        Iy = Ix if x == y else calc_reindexing_tensor(y, L)
        Py = jnp.einsum('yir,rd->yid', Iy, rel_columns)
        Sy = jnp.einsum('ndxy,yid->nixy', q4, Py)
        rel_pos_out = jnp.einsum('nixy,nexi->nexy', Sy, Yh)
        out = content_out + rel_pos_out
        out = out.reshape(b, H * DK, x, y)
        return jnp.einsum('bcxy,oc->boxy', out, w_out) + b_out[None, :, None, None]

    def _gn(v, G=32, eps=1e-5):
        B_, C_, H_, W_ = v.shape
        g = v.reshape(B_, G, C_ // G, H_, W_)
        m = jnp.mean(g, axis=(2, 3, 4), keepdims=True)
        s = jnp.var(g, axis=(2, 3, 4), keepdims=True)
        return ((g - m) / jnp.sqrt(s + eps)).reshape(v.shape)

    def _ln_c(v, eps=1e-6):
        m = jnp.mean(v, axis=1, keepdims=True)
        s = jnp.var(v, axis=1, keepdims=True)
        return (v - m) / jnp.sqrt(s + eps)

    def _ln_t(v, eps=1e-5):
        m = jnp.mean(v, axis=-1, keepdims=True)
        s = jnp.var(v, axis=-1, keepdims=True)
        return (v - m) / jnp.sqrt(s + eps)

    def _to_tokens(v):
        B_, C_, H_, W_ = v.shape
        return v.reshape(B_, C_, H_ * W_).transpose(0, 2, 1)
    def _from_tokens(t, like):
        B_, C_, H_, W_ = like.shape
        return t.transpose(0, 2, 1).reshape(B_, C_, H_, W_)

    x = x + _L0_conv_ref(_gn(x), L0_conv_w_qkv, L0_conv_w_out, L0_conv_b_out, L0_conv_rel_rows, L0_conv_rel_columns, L0_conv_bn_gamma, L0_conv_bn_beta)
    return x


_drawn_inputs = setup_inputs


def setup_inputs(seed=0):
    import zlib

    import numpy as np

    out = dict(_drawn_inputs(seed))
    spreads = {'L0_conv_b_out': (0.0, 0.8), 'L0_conv_bn_gamma': (1.0, 0.2), 'L0_conv_bn_beta': (0.0, 0.1)}
    factors = {}
    for name, (base, spread) in spreads.items():
        noise = np.random.default_rng([zlib.crc32(name.encode()), seed]).standard_normal(out[name].shape)
        drawn = base * np.exp(spread * noise) if base else spread * noise
        out[name] = jnp.asarray(drawn.astype(out[name].dtype))
    for name, factor in factors.items():
        out[name] = (out[name] * factor).astype(out[name].dtype)
    return out
```

```python
from contextlib import ExitStack

import concourse.bass as bass
from concourse import mybir

F32 = mybir.dt.float32
F16 = mybir.dt.float16
ALU = mybir.AluOpType
ACT = mybir.ActivationFunctionType
AX = mybir.AxisListType

P = 128
GN_EPS = 1e-5
BN_EPS = 1e-5
TINY = 1e-30
BANKS = 5
BANK = 512
YST = 2
YSQ = 2


def attention_kernel(nc, x, w_qkv_t, w_out_t, b_out, rel_rows_t, rel_cols_t, gamma, beta,
                     ident_in, group_in, parity_in, out):
    NB, C, H, W = x.shape
    CC = C // P
    DK = rel_rows_t.shape[0]
    HID = w_out_t.shape[0]
    HP = HID // P
    PIX = H * W
    HALF = W // 2
    NT = NB * HP
    NREL = 2 * W - 1
    assert DK == 64 and H == 64 and W == 64 and CC == 2 and HP == 4
    x_chunks = x.rearrange("b (c p) h w -> b c p (h w)", p=P)
    out_chunks = out.rearrange("b (c p) h w -> b c p (h w)", p=P)
    N_BN = float(NB * (HID // DK) * PIX)

    q_dram = nc.dram_tensor("q_scratch", (NT, 2, DK, 2, 2, H * HALF), F16, kind="Internal").ap()
    y_dram = nc.dram_tensor("y_scratch", (NT, 2, HALF, 2, H, DK), F32, kind="Internal").ap()
    c_dram = nc.dram_tensor("ctx_scratch", (NT, P, DK), F32, kind="Internal").ap()

    TERMS = ((0, 0), (0, 1), (1, 0))

    KV, Q, SX, YH = 2 * 8, 8, 8, 8
    fills = []
    for hp in range(HP):
        if hp == 0:
            fills += [("kv", 0, i) for i in range(KV)]
        if hp > 0:
            fills += [("yh", hp - 1, i) for i in range(YH)]
        fills += [("q", hp, i) for i in range(Q)]
        fills += [("sx", hp, i) for i in range(SX)]
        if hp + 1 < HP:
            fills += [("kv", hp + 1, i) for i in range(KV)]
    fills += [("yh", HP - 1, i) for i in range(YH)]
    NF = len(fills)
    assert NF % BANKS == 0
    pos = {f: n for n, f in enumerate(fills)}
    after_kv = {hp: pos["kv", hp, KV - 1] for hp in range(HP)}

    with ExitStack() as top:
        def sb(name, shape, dt, c=top):
            return c.enter_context(nc.sbuf_tensor(name, list(shape), dt))

        def ps(name, shape, c=top):
            return c.enter_context(nc.psum_tensor(name, list(shape), F32))

        def sem(name, c=top):
            return c.enter_context(nc.semaphore(name))

        bank = ps("bank", [P, BANKS, BANK])
        ctx_ps = ps("ctx_ps", [P, BANK])
        small_ps = ps("small_ps", [P, BANK])
        gn_ps = ps("gn_ps", [P, BANK])

        scale_all = sb("scale_all", [P, 4], F32)
        inv_all = sb("inv_all", [P, 4], F32)
        factors = sb("factors", [P, 4], F32)
        rc_hi = sb("rc_hi", [P, 2 * P], F16)
        rc_lo = sb("rc_lo", [P, 2 * P], F16)
        ones = sb("ones", [P, P], F32)
        parity = sb("parity", [P, 2], F32)
        minus_half = sb("minus_half", [P, DK], F32)
        acc = sb("acc", [P, 2, BANK], F32)

        p1 = ExitStack()
        w_hi = sb("w_hi", [P, CC, 3 * HID], F16, p1)
        w_lo = sb("w_lo", [P, CC, 3 * HID], F16, p1)
        rr_hi = sb("rr_hi", [P, 2 * P], F16, p1)
        rr_lo = sb("rr_lo", [P, 2 * P], F16, p1)
        ident = sb("ident", [P, P], F32, p1)
        group = sb("group", [P, P], F32, p1)

        with ExitStack() as st, nc.Block() as block:
            w_f = sb("w_f", [P, CC, 3 * HID], F32, st)
            rr_f = sb("rr_f", [P, 2 * P], F32, st)
            rc_f = sb("rc_f", [P, 2 * P], F32, st)
            wo_f = sb("wo_f", [P, HP, C], F32, st)
            mx = sb("mx", [P, 4], F32, st)
            rel_in = sb("rel_in", [P, 2, NREL], F32, st)
            s_zero = sem("s_zero", st)
            s_ld = sem("s_ld", st)
            s_mx = sem("s_mx", st)
            s_all = sem("s_all", st)
            s_sc = sem("s_sc", st)

            @block.sync
            def _(sp):
                sp.dma_start(w_f[:, :, :], w_qkv_t.rearrange("(a p) n -> p a n", p=P)).then_inc(s_ld, 16)
                sp.dma_start(wo_f[:, :, :], w_out_t.rearrange("(a p) n -> p a n", p=P)).then_inc(s_ld, 16)
                sp.dma_start(ident[:, :], ident_in[:, :]).then_inc(s_ld, 16)
                sp.dma_start(group[:, :], group_in[:, :]).then_inc(s_ld, 16)
                sp.dma_start(parity[:, :], parity_in[:, :]).then_inc(s_ld, 16)
                for g in range(2):
                    sp.dma_start(rel_in[g * 64:g * 64 + 64, 0, :], rel_rows_t[:, :]).then_inc(s_ld, 16)
                    sp.dma_start(rel_in[g * 64:g * 64 + 64, 1, :], rel_cols_t[:, :]).then_inc(s_ld, 16)
                sp.wait_ge(s_ld, 144)

            @block.gpsimd
            def _(pool):
                pool.wait_ge(s_mx, 4)
                pool.partition_all_reduce(scale_all[:, :], mx[:, :], P, bass.bass_isa.ReduceOp.max).then_inc(s_all, 1)
                pool.memset(minus_half[:, :], -0.5).then_inc(s_all, 1)

            @block.vector
            def _(dve):
                dve.memset(rr_f[:, :], 0.0).then_inc(s_zero, 1)
                dve.memset(rc_f[:, :], 0.0).then_inc(s_zero, 1)
                dve.memset(ones[:, :], 1.0)
                dve.wait_ge(s_ld, 144)
                dve.wait_ge(s_zero, 2)
                for g in range(2):
                    s = slice(g * 64, g * 64 + 64)
                    dve.tensor_copy(rr_f[s, g:2 * NREL:2], rel_in[s, 0, :]).then_inc(s_zero, 1)
                    dve.tensor_copy(rc_f[s, g:2 * NREL:2], rel_in[s, 1, :]).then_inc(s_zero, 1)
                dve.wait_ge(s_zero, 6)
                for n, t in enumerate((w_f[:, :, :], rr_f[:, :], rc_f[:, :], wo_f[:, :, :])):
                    axis = AX.XY if n in (0, 3) else AX.X
                    dve.tensor_reduce(mx[:, n:n + 1], t, axis, ALU.max,
                                      apply_absolute_value=True).then_inc(s_mx, 1)
                dve.wait_ge(s_all, 1)
                dve.tensor_scalar(scale_all[:, :], scale_all[:, :], TINY, None, ALU.max).then_inc(s_sc, 1)
                dve.wait_ge(s_sc, 1)
                dve.reciprocal(inv_all[:, :], scale_all[:, :]).then_inc(s_sc, 1)
                dve.tensor_tensor(factors[:, 1:2], scale_all[:, 0:1], scale_all[:, 0:1], ALU.mult).then_inc(s_sc, 1)
                dve.tensor_tensor(factors[:, 2:3], scale_all[:, 0:1], scale_all[:, 2:3], ALU.mult).then_inc(s_sc, 1)
                dve.wait_ge(s_sc, 4)
                dve.tensor_tensor(factors[:, 0:1], scale_all[:, 0:1], inv_all[:, 2:3], ALU.mult).then_inc(s_sc, 1)
                dve.tensor_tensor(factors[:, 1:2], factors[:, 1:2], scale_all[:, 1:2], ALU.mult).then_inc(s_sc, 1)
                dve.tensor_tensor(factors[:, 2:3], factors[:, 2:3], scale_all[:, 3:4], ALU.mult).then_inc(s_sc, 1)
                n = 7
                for src, hi, lo, k in ((w_f, w_hi, w_lo, 0), (rr_f, rr_hi, rr_lo, 1), (rc_f, rc_hi, rc_lo, 2)):
                    s, h, l = (t[:, :, :] if k == 0 else t[:, :] for t in (src, hi, lo))
                    dve.tensor_scalar(s, s, inv_all[:, k:k + 1], None, ALU.mult).then_inc(s_sc, 1)
                    dve.wait_ge(s_sc, n + 1)
                    dve.tensor_copy(h, s).then_inc(s_sc, 1)
                    dve.wait_ge(s_sc, n + 2)
                    dve.tensor_tensor(l, s, h, ALU.subtract).then_inc(s_sc, 1)
                    n += 3
                dve.wait_ge(s_sc, n)

        with p1, nc.Block() as block:
            x_f = sb("x_f", [P, CC, PIX], F32, p1)
            x_hi = sb("x_hi", [P, CC, PIX], F16, p1)
            x_lo = sb("x_lo", [P, CC, PIX], F16, p1)
            k_f = sb("k_f", [P, HALF, P], F32, p1)
            p_hi = sb("p_hi", [P, HALF, P], F16, p1)
            p_lo = sb("p_lo", [P, HALF, P], F16, p1)
            VW = P + 2
            v_hi = sb("v_hi", [P, 2, HALF, VW], F16, p1)
            v_lo = sb("v_lo", [P, 2, HALF, VW], F16, p1)
            q_hi = sb("q_hi", [P, 2, H, HALF], F16, p1)
            q_lo = sb("q_lo", [P, 2, H, HALF], F16, p1)
            sx_hi = sb("sx_hi", [P, 2 * HALF, 2, H], F16, p1)
            sx_lo = sb("sx_lo", [P, 2 * HALF, 2, H], F16, p1)
            yst = sb("yst", [P, YST, BANK], F32, p1)
            ysq = sb("ysq", [P, YSQ, BANK], F32, p1)
            kmax_halves = sb("kmax_halves", [P, 2, P], F32, p1)
            kmax = sb("kmax", [P, P], F32, p1)
            diag = sb("diag", [P, P], F32, p1)
            negmax = sb("negmax", [P, P], F32, p1)
            colmax = sb("colmax", [P, 1], F32, p1)
            cden = sb("cden", [P, 1], F32, p1)
            cst = sb("cst", [P, DK], F32, p1)
            bn6 = sb("bn6", [P, CC, 8, 6], F32, p1)
            mv = sb("mv", [P, CC, 2], F32, p1)
            spare = sb("spare", [P, 2], F32, p1)
            gs = sb("gs", [P, CC, 2], F32, p1)
            rstd = sb("rstd", [P, CC], F32, p1)
            nbias = sb("nbias", [P, CC], F32, p1)

            filled = sem("filled", p1)
            hi_done = sem("hi_done", p1)
            freed = sem("freed", p1)
            x_in = sem("x_in", p1)
            bn_done = sem("bn_done", p1)
            gn_sum = sem("gn_sum", p1)
            gn_root = sem("gn_root", p1)
            x_norm = sem("x_norm", p1)
            x_hi_done = sem("x_hi_done", p1)
            x_lo_a = sem("x_lo_a", p1)
            x_lo_b = sem("x_lo_b", p1)
            kmax_done = sem("kmax_done", p1)
            small = sem("small", p1)
            max_done = sem("max_done", p1)
            shifted = sem("shifted", p1)
            exp_done = sem("exp_done", p1)
            p_hi_done = sem("p_hi_done", p1)
            p_lo_done = sem("p_lo_done", p1)
            ctx_done = sem("ctx_done", p1)
            ctx_out = sem("ctx_out", p1)
            ctx_st = sem("ctx_st", p1)
            q_st = sem("q_st", p1)
            y_st = [sem(f"y_st{s}", p1) for s in range(YST)]
            sums = sem("sums", p1)
            init = sem("init", p1)

            NXC = 4
            XC = PIX // NXC
            NBN = 16 + 1 + 2 + 2 + 1 + 4 + 2

            def evacuated(b, key):
                return b * NF + (BANKS + 1 + pos[key])

            xh_kv = [t[:, :, :].rearrange("p c (k y) -> p c y k", y=HALF) for t in (x_hi, x_lo)]
            xh_q = [t[:, :, :].rearrange("p c (x g y) -> p c g x y", g=2, y=HALF) for t in (x_hi, x_lo)]
            w_kv = [t[:, :, HID:3 * HID].rearrange("p c (t n) -> p c t n", t=2) for t in (w_hi, w_lo)]
            @block.sync
            def _(sp):
                def load_x(index):
                    for c in range(CC):
                        sp.dma_start(x_f[:, c, :], x_chunks[index, c]).then_inc(x_in, 16)

                sp.sem_inc(q_st, 64)
                sp.sem_inc(ctx_st, 16)
                for s in range(YST):
                    sp.sem_inc(y_st[s], 32)
                load_x(0)
                with sp.Fori(0, NB) as b:
                    sp.wait_ge(x_lo_a, (b + 1) * NXC)
                    sp.wait_ge(x_lo_b, (b + 1) * NXC)
                    load_x((b + 1) % NB)
                    for hp in range(HP):
                        t = b * HP + hp
                        sp.wait_ge(freed, evacuated(b, ("q", hp, Q - 1)))
                        for part, src in enumerate((q_hi, q_lo)):
                            for g in range(2):
                                sp.dma_start(q_dram[t].rearrange("h d l g n -> l g d h n")[part, g],
                                             src[g * 64:g * 64 + 64, :, :, :].rearrange("p h x y -> p h (x y)")
                                             ).then_inc(q_st, 16)
                        for i in range(YH):
                            sp.wait_ge(freed, evacuated(b, ("yh", hp, i)))
                            for g in range(2):
                                sp.dma_start(
                                    y_dram[t, g, 4 * i:4 * i + 4].rearrange("y h x e -> x (y h) e"),
                                    yst[g * 64:g * 64 + 64, i % YST, :].rearrange("p (y e) -> p y e", e=DK)
                                    ).then_inc(y_st[i % YST], 16)
                        sp.wait_ge(ctx_out, t * 3 + 4)
                        sp.dma_start(c_dram[t], cst[:, :]).then_inc(ctx_st, 16)
                sp.wait_ge(q_st, 64 * (NT + 1))
                sp.wait_ge(ctx_st, 16 * (NT + 1))
                for s in range(YST):
                    sp.wait_ge(y_st[s], 32 * (NT * YH // YST + 1))
                sp.wait_ge(x_in, 16 * CC * (NB + 1))

            @block.tensor
            def _(pe):
                def pairs(outs, lhs, rhs, first, last, **kw):
                    for n, (a, m) in enumerate(TERMS):
                        mm = pe.matmul(outs, lhs[a], rhs[m], start=first and n == 0,
                                       stop=last and n == 2, **kw)
                    return mm

                def gn_groups(nth):
                    pe.wait_ge(bn_done, nth * NBN + 21)
                    pe.matmul(gn_ps[:, 0:4], group[:, :], mv[:, :, :].rearrange("p c k -> p (c k)"),
                              start=True, stop=True).then_inc(gn_sum, 1)

                pe.sem_inc(ctx_done, 1)
                gn_groups(0)
                with pe.Fori(0, NB) as b:
                    for n, (kind, hp, i) in enumerate(fills):
                        t = b * HP + hp
                        r = n % BANKS
                        pe.wait_ge(freed, b * NF + (n + 1))
                        if kind == "kv":
                            if hp == 0 and i == 0:
                                pe.wait_ge(x_lo_a, (b + 1) * NXC)
                                pe.wait_ge(x_lo_b, (b + 1) * NXC)
                            for j in range(2):
                                y2 = 2 * i + j
                                for c in range(CC):
                                    mm = pairs(bank[:, r, j * 256:j * 256 + 256],
                                               [s[:, c, y2] for s in xh_kv],
                                               [s[:, c, :, hp * P:hp * P + P] for s in w_kv],
                                               c == 0, c == CC - 1)
                        elif kind == "q":
                            x0, h2 = (i // 2) * 16, i % 2
                            for c in range(CC):
                                for k, (a, m) in enumerate(TERMS):
                                    for g in range(2):
                                        ww = (w_hi, w_lo)[a][:, c, hp * P + h2 * 64:hp * P + h2 * 64 + 64]
                                        mm = pe.matmul(bank[g * 64:g * 64 + 64, r, :], ww,
                                                       xh_q[m][:, c, g, x0:x0 + 16, :],
                                                       start=(c == 0 and k == 0), stop=(c == CC - 1 and k == 2))
                        elif kind == "sx":
                            if i % 2 == 0:
                                pe.wait_ge(freed, evacuated(b, ("q", hp, i + 1)))
                            for j in range(8):
                                xx = 8 * i + j
                                mm = pairs(bank[:, r, j * 64:j * 64 + 64],
                                           [s[:, 2 * (H - 1 - xx):2 * (H - 1 - xx) + P] for s in (rr_hi, rr_lo)],
                                           [s[:, :, xx, :] for s in (q_hi, q_lo)], True, True)
                        else:
                            if i == 0:
                                pe.wait_ge(freed, evacuated(b, ("sx", hp, SX - 1)))
                            for j in range(4):
                                y2 = 4 * i + j
                                for h2 in range(2):
                                    mm = pairs(bank[:, r, (2 * j + h2) * 64:(2 * j + h2) * 64 + 64],
                                               [s[:, h2 * HALF + y2, :, :].rearrange("p g x -> p (g x)") for s in (sx_hi, sx_lo)],
                                               [s[:, hp % 2, y2, h2 * 64:h2 * 64 + 64] for s in (v_hi, v_lo)],
                                               True, True)
                        mm.then_inc(filled, 1)
                        for h in range(HP):
                            if n == after_kv[h] + 2:
                                pe.wait_ge(kmax_done, (b * HP + h) * 3 + 3)
                                pe.transpose(small_ps[:, 0:P], kmax[:, :], ident[:, :]).then_inc(small, 1)
                            if n == after_kv[h] + 5:
                                pe.wait_ge(max_done, (b * HP + h) * 3 + 2)
                                pe.matmul(small_ps[:, P:2 * P], ones[:, :], diag[:, :],
                                          start=True, stop=True).then_inc(small, 1)
                        if (kind, i) == ("yh", YH - 1):
                            pe.wait_ge(p_lo_done, t * 4 + 5)
                            pe.wait_ge(ctx_out, t * 3 + 1)
                            for y2 in range(HALF):
                                for k, (a, m) in enumerate(TERMS):
                                    mm = pe.matmul(ctx_ps[:, 0:VW], (p_hi, p_lo)[a][:, y2, :],
                                                   (v_hi, v_lo)[m][:, hp % 2, y2, :],
                                                   start=(y2 == 0 and k == 0), stop=(y2 == HALF - 1 and k == 2))
                            mm.then_inc(ctx_done, 1)
                        if (kind, hp, i) == ("q", 2, 5):
                            gn_groups(b + 1)

            @block.scalar
            def _(act):
                def split_x(nth, c, piece):
                    act.wait_ge(x_norm, nth * 8 + c * NXC + piece + 1)
                    s = slice(piece * XC, piece * XC + XC)
                    act.activation(x_hi[:, c, s], x_f[:, c, s], ACT.Copy).then_inc(x_hi_done, 1)

                for m in range(8):
                    split_x(0, m // NXC, m % NXC)
                act.wait_ge(init, 4)
                with act.Fori(0, NB) as b:
                    for n, (kind, hp, i) in enumerate(fills):
                        t = b * HP + hp
                        src = bank[:, n % BANKS, :]
                        if kind == "kv" and i == 0:
                            act.wait_ge(p_lo_done, t * 4 + 1)
                        if kind == "q" and i == 0:
                            act.wait_ge(q_st, t * 64 + 64)
                        if kind == "yh":
                            act.wait_ge(sums, (t * YH + i) * 2 + 4)
                        act.wait_ge(filled, b * NF + (n + 1))
                        if kind == "kv":
                            v = src.rearrange("p (j t n) -> p j t n", j=2, t=2)
                            act.activation(k_f[:, 2 * i:2 * i + 2, :], v[:, :, 0, :], ACT.Copy)
                            act.activation(v_hi[:, hp % 2, 2 * i:2 * i + 2, 0:P], v[:, :, 1, :],
                                           ACT.Copy).then_inc(hi_done, 1)
                        elif kind == "q":
                            x0, h2 = (i // 2) * 16, i % 2
                            act.activation(q_hi[:, h2, x0:x0 + 16, :].rearrange("p x y -> p (x y)"), src,
                                           ACT.Copy).then_inc(hi_done, 1)
                        elif kind == "sx":
                            for g in range(2):
                                o = act.activation(sx_hi[:, :, g, 8 * i:8 * i + 8],
                                                   src.rearrange("p (x h) -> p h x", x=8),
                                                   ACT.Copy, scale=parity[:, g:g + 1])
                            o.then_inc(hi_done, 1)
                        else:
                            act.activation(ysq[:, i % YSQ, :], src, ACT.Square).then_inc(hi_done, 1)
                        for h in range(HP):
                            j = n - after_kv[h] - 8
                            if 0 <= j < 4:
                                c = (b * HP + h) * 4 + (j + 1)
                                act.wait_ge(shifted, c)
                                kk = k_f[:, 8 * j:8 * j + 8, :]
                                act.activation(kk, kk, ACT.Exp, scale=scale_all[:, 0:1]).then_inc(exp_done, 1)
                            j = n - after_kv[h] - 10
                            if 0 <= j < 4:
                                c = (b * HP + h) * 4 + (j + 1)
                                act.wait_ge(exp_done, c)
                                act.wait_ge(ctx_done, b * HP + (h + 1))
                                act.activation(p_hi[:, 8 * j:8 * j + 8, :], k_f[:, 8 * j:8 * j + 8, :],
                                               ACT.Copy).then_inc(p_hi_done, 1)
                        if kind in ("sx", "yh") and hp == HP - 1:
                            m = n - pos["sx", HP - 1, 0]
                            if m < 8:
                                split_x(b + 1, m // NXC, m % NXC)

            def context_out(dve, t):
                dve.wait_ge(ctx_done, t + 2)
                dve.wait_ge(ctx_st, t * 16 + 16)
                dve.reciprocal(cden[:, :], ctx_ps[:, P:P + 1]).then_inc(ctx_out, 1)
                dve.wait_ge(ctx_out, t * 3 + 2)
                for g in range(2):
                    s = slice(g * 64, g * 64 + 64)
                    dve.tensor_scalar(cst[s, :], ctx_ps[s, g * 64:g * 64 + 64], cden[s, 0:1], factors[s, 0:1],
                                      ALU.mult, ALU.mult).then_inc(ctx_out, 1)

            @block.vector
            def _(dve):
                dve.memset(v_hi[:, 0, :, P:VW], 1.0).then_inc(init, 1)
                dve.memset(v_hi[:, 1, :, P:VW], 1.0).then_inc(init, 1)
                dve.memset(v_lo[:, 0, :, P:VW], 0.0).then_inc(init, 1)
                dve.memset(v_lo[:, 1, :, P:VW], 0.0).then_inc(init, 1)
                dve.sem_inc(freed, BANKS)
                dve.sem_inc(ctx_out, 1)
                dve.sem_inc(p_lo_done, 1)

                def gn_stats(nth, k):
                    c, j = k // 8, k % 8
                    if k % 8 == 0:
                        dve.wait_ge(x_in, nth * 16 * CC + 16 * CC)
                    dve.bn_stats(bn6[:, c, j, :], x_f[:, c, j * 512:j * 512 + 512]).then_inc(bn_done, 1)

                def gn_channels(nth):
                    base = nth * NBN
                    dve.wait_ge(bn_done, base + 16)
                    dve.memset(spare[:, 0:2], 0.0).then_inc(bn_done, 1)
                    for c in range(CC):
                        dve.bn_aggr(mv[:, c, :], bn6[:, c, :, :].rearrange("p a b -> p (a b)")).then_inc(bn_done, 1)
                    dve.wait_ge(bn_done, base + 19)
                    for c in range(CC):
                        dve.scalar_tensor_tensor(mv[:, c, 1:2], mv[:, c, 0:1], mv[:, c, 0:1], mv[:, c, 1:2],
                                                 ALU.mult, ALU.add).then_inc(bn_done, 1)

                def gn_scale(nth):
                    base = nth * NBN + 21
                    dve.wait_ge(gn_sum, nth + 1)
                    dve.tensor_copy(gs[:, :, :].rearrange("p c k -> p (c k)"), gn_ps[:, 0:4]).then_inc(bn_done, 1)
                    dve.wait_ge(bn_done, base + 1)
                    dve.tensor_tensor(rstd[:, :], gs[:, :, 0], gs[:, :, 0], ALU.mult).then_inc(bn_done, 1)
                    dve.wait_ge(bn_done, base + 2)
                    dve.tensor_tensor(rstd[:, :], gs[:, :, 1], rstd[:, :], ALU.subtract).then_inc(bn_done, 1)
                    dve.wait_ge(bn_done, base + 3)
                    dve.tensor_scalar(rstd[:, :], rstd[:, :], 0.0, None, ALU.max).then_inc(bn_done, 1)
                    dve.wait_ge(bn_done, base + 4)
                    dve.tensor_scalar(rstd[:, :], rstd[:, :], GN_EPS, None, ALU.add).then_inc(bn_done, 1)

                def gn_bias(nth):
                    base = nth * NBN + 21
                    dve.wait_ge(gn_root, nth + 1)
                    dve.tensor_tensor(nbias[:, :], gs[:, :, 0], rstd[:, :], ALU.mult).then_inc(bn_done, 1)
                    dve.wait_ge(bn_done, base + 6)
                    dve.tensor_scalar(nbias[:, :], nbias[:, :], -1.0, None, ALU.mult).then_inc(bn_done, 1)

                def gn_apply(nth, k):
                    c, j = k // NXC, k % NXC
                    if k == 0:
                        dve.wait_ge(bn_done, nth * NBN + NBN)
                    s = x_f[:, c, j * XC:j * XC + XC]
                    dve.tensor_scalar(s, s, rstd[:, c:c + 1], nbias[:, c:c + 1],
                                      ALU.mult, ALU.add).then_inc(x_norm, 1)

                def split_x(nth, j):
                    dve.wait_ge(x_hi_done, nth * 8 + (j + 1))
                    s = slice(j * XC, j * XC + XC)
                    dve.tensor_tensor(x_lo[:, 0, s], x_f[:, 0, s], x_hi[:, 0, s], ALU.subtract).then_inc(x_lo_a, 1)

                for k in range(16):
                    gn_stats(0, k)
                gn_channels(0)
                gn_scale(0)
                gn_bias(0)
                for k in range(8):
                    gn_apply(0, k)
                for j in range(NXC):
                    split_x(0, j)
                with dve.Fori(0, NB) as b:
                    for n, (kind, hp, i) in enumerate(fills):
                        t = b * HP + hp
                        src = bank[:, n % BANKS, :]
                        if kind == "yh":
                            dve.wait_ge(y_st[i % YST], (t * (YH // YST) + (i // YST + 1)) * 32)
                            dve.wait_ge(sums, (t * YH + i) * 2 + 4)
                        dve.wait_ge(hi_done, b * NF + (n + 1))
                        if kind == "kv":
                            v = src.rearrange("p (j t n) -> p j t n", j=2, t=2)
                            dve.tensor_tensor(v_lo[:, hp % 2, 2 * i:2 * i + 2, 0:P], v[:, :, 1, :],
                                              v_hi[:, hp % 2, 2 * i:2 * i + 2, 0:P], ALU.subtract).then_inc(freed, 1)
                            if i % 8 == 7:
                                j = i // 8
                                dve.tensor_reduce(kmax_halves[:, j, :],
                                                  k_f[:, 16 * j:16 * j + 16, :].rearrange("p y c -> p c y"),
                                                  AX.X, ALU.max).then_inc(kmax_done, 1)
                            if i == KV - 1:
                                dve.wait_ge(kmax_done, t * 3 + 2)
                                dve.tensor_reduce(kmax[:, :], kmax_halves[:, :, :].rearrange("p y c -> p c y"),
                                                  AX.X, ALU.max).then_inc(kmax_done, 1)
                            if hp == 2:
                                gn_stats(b + 1, i)
                            if hp == 3 and i < 8:
                                gn_apply(b + 1, i)
                        elif kind == "q":
                            x0, h2 = (i // 2) * 16, i % 2
                            dve.tensor_tensor(q_lo[:, h2, x0:x0 + 16, :].rearrange("p x y -> p (x y)"), src,
                                              q_hi[:, h2, x0:x0 + 16, :].rearrange("p x y -> p (x y)"),
                                              ALU.subtract).then_inc(freed, 1)
                            if (hp, i) == (2, 3):
                                gn_channels(b + 1)
                            if (hp, i) == (2, 7):
                                gn_scale(b + 1)
                        elif kind == "sx":
                            if (hp, i) == (2, 4):
                                gn_bias(b + 1)
                            for g in range(2):
                                s = slice(8 * i, 8 * i + 8)
                                o = dve.scalar_tensor_tensor(sx_lo[:, :, g, s],
                                                             src.rearrange("p (x h) -> p h x", x=8),
                                                             parity[:, g:g + 1], sx_hi[:, :, g, s],
                                                             ALU.mult, ALU.subtract)
                            o.then_inc(freed, 1)
                        else:
                            dve.tensor_copy(yst[:, i % YST, :], src).then_inc(freed, 1)
                        for h in range(HP):
                            th = b * HP + h
                            if n == after_kv[h] + 3:
                                dve.wait_ge(small, th * 2 + 1)
                                dve.tensor_reduce(colmax[:, :], small_ps[:, 0:P], AX.X, ALU.max,
                                                  negate=True).then_inc(max_done, 1)
                                dve.wait_ge(max_done, th * 3 + 1)
                                dve.tensor_scalar(diag[:, :], ident[:, :], colmax[:, 0:1], None,
                                                  ALU.mult).then_inc(max_done, 1)
                            if n == after_kv[h] + 6:
                                dve.wait_ge(small, th * 2 + 2)
                                dve.tensor_copy(negmax[:, :], small_ps[:, P:2 * P]).then_inc(max_done, 1)
                            j = n - after_kv[h] - 11
                            if 0 <= j < 4:
                                dve.wait_ge(p_hi_done, th * 4 + (j + 1))
                                s = slice(8 * j, 8 * j + 8)
                                dve.tensor_tensor(p_lo[:, s, :], k_f[:, s, :], p_hi[:, s, :],
                                                  ALU.subtract).then_inc(p_lo_done, 1)
                        if (kind, i) == ("q", 4) and hp > 0:
                            context_out(dve, b * HP + (hp - 1))
                        if (kind, hp) in (("sx", HP - 1), ("yh", HP - 1)):
                            m = n - pos["sx", HP - 1, 0] - 1
                            if 0 <= m < NXC:
                                split_x(b + 1, m)
                    context_out(dve, b * HP + (HP - 1))

            @block.gpsimd
            def _(pool):
                def split_x(nth, j):
                    pool.wait_ge(x_hi_done, nth * 8 + (NXC + j + 1))
                    s = slice(j * XC, j * XC + XC)
                    pool.tensor_tensor(x_lo[:, 1, s], x_f[:, 1, s], x_hi[:, 1, s], ALU.subtract).then_inc(x_lo_b, 1)

                def gn_power(nth):
                    pool.wait_ge(bn_done, nth * NBN + 26)
                    pool.tensor_tensor(rstd[:, :], rstd[:, :], minus_half[:, 0:CC], ALU.pow).then_inc(gn_root, 1)

                def shift(t, j):
                    if j == 0:
                        pool.wait_ge(max_done, t * 3 + 3)
                    kk = k_f[:, 8 * j:8 * j + 8, :]
                    pool.tensor_tensor(kk, kk, negmax[:, :].unsqueeze(1).to_broadcast([P, 8, P]),
                                       ALU.add).then_inc(shifted, 1)

                def take_sums(b, hp, i):
                    u = (b * HP + hp) * YH + i
                    pool.wait_ge(freed, evacuated(b, ("yh", hp, i)))
                    pool.wait_ge(sums, u * 2 + 5)
                    pool.tensor_tensor(acc[:, 0, :], acc[:, 0, :], yst[:, i % YST, :], ALU.add).then_inc(sums, 1)
                    pool.wait_ge(sums, u * 2 + 6)
                    pool.tensor_tensor(acc[:, 1, :], acc[:, 1, :], ysq[:, i % YSQ, :], ALU.add).then_inc(sums, 1)

                pool.memset(acc[:, :, :], 0.0).then_inc(sums, 6)
                gn_power(0)
                for j in range(NXC):
                    split_x(0, j)
                with pool.Fori(0, NB) as b:
                    for hp in range(HP):
                        if hp > 0:
                            for i in range(YH - 2):
                                take_sums(b, hp - 1, i)
                        for j in range(4):
                            shift(b * HP + hp, j)
                        if hp > 0:
                            for i in range(YH - 2, YH):
                                take_sums(b, hp - 1, i)
                        if hp == 2:
                            gn_power(b + 1)
                    for j in range(NXC):
                        split_x(b + 1, j)
                    for i in range(YH):
                        take_sums(b, HP - 1, i)

        SY, RO, PR = 8, 8, CC * 8
        fills2 = [("sy", 0, i) for i in range(SY)]
        for hp in range(HP):
            for i in range(RO):
                if hp + 1 < HP:
                    fills2.append(("sy", hp + 1, i))
                fills2.append(("ro", hp, i))
        fills2 += [("pr", 0, i) for i in range(PR)]
        NF2 = len(fills2)
        assert NF2 % BANKS == 0
        pos2 = {f: n for n, f in enumerate(fills2)}
        YC = 4
        XY = H // YC
        XS = 4

        with ExitStack() as p2, nc.Block() as block:
            q2 = sb("q2", [P, 2, 2, 2, H, HALF], F16, p2)
            y_f = sb("y_f", [P, YC, XY, DK], F32, p2)
            yb_hi = sb("yb_hi", [P, H, 2, DK], F16, p2)
            yb_lo = sb("yb_lo", [P, H, 2, DK], F16, p2)
            sy_hi = sb("sy_hi", [P, 2, H, W], F16, p2)
            sy_lo = sb("sy_lo", [P, 2, H, W], F16, p2)
            o_hi = sb("o_hi", [P, HP, PIX], F16, p2)
            o_lo = sb("o_lo", [P, HP, PIX], F16, p2)
            wo_f = sb("wo_f2", [P, HP, C], F32, p2)
            wo_hi = sb("wo_hi", [P, HP, C], F16, p2)
            wo_lo = sb("wo_lo", [P, HP, C], F16, p2)
            c_f = sb("c_f", [P, DK], F32, p2)
            cb_hi = sb("cb_hi", [P, 2, 2, DK], F16, p2)
            cb_lo = sb("cb_lo", [P, 2, 2, DK], F16, p2)
            x_res = sb("x_res", [P, XS, BANK], F32, p2)
            bias = sb("bias", [P, CC], F32, p2)
            gam = sb("gam", [P, DK], F32, p2)
            bet = sb("bet", [P, DK], F32, p2)
            st = sb("st", [P, 2, DK], F32, p2)
            mean = sb("mean", [P, DK], F32, p2)
            var = sb("var", [P, DK], F32, p2)
            y_mul = sb("y_mul", [P, DK], F32, p2)
            y_add = sb("y_add", [P, DK], F32, p2)

            filled = sem("filled2", p2)
            hi_done = sem("hi_done2", p2)
            freed = sem("freed2", p2)
            const_in = sem("const_in", p2)
            stat = sem("stat", p2)
            stat_ps = sem("stat_ps", p2)
            root = sem("root", p2)
            init = sem("init2", p2)
            q_in = [sem(f"q_in{s}", p2) for s in range(2)]
            y_in = [sem(f"y_in{s}", p2) for s in range(YC)]
            c_in = sem("c_in", p2)
            x_in = [sem(f"xr_in{s}", p2) for s in range(XS)]
            y_norm = sem("y_norm", p2)
            yb_hi_done = sem("yb_hi_done", p2)
            yb_lo_done = sem("yb_lo_done", p2)
            cb_hi_done = sem("cb_hi_done", p2)
            cb_lo_done = sem("cb_lo_done", p2)
            out_st = [sem(f"out_st{s}", p2) for s in range(XS)]
            NSTAT = 12

            def done2(b, key):
                return b * NF2 + (NF2 + BANKS + 1 + pos2[key])

            @block.sync
            def _(sp):
                sp.dma_start(gam[:, :], gamma.unsqueeze(0).to_broadcast([P, DK])).then_inc(const_in, 16)
                sp.dma_start(bet[:, :], beta.unsqueeze(0).to_broadcast([P, DK])).then_inc(const_in, 16)
                sp.dma_start(bias[:, :], b_out.rearrange("(c p) -> p c", p=P),
                             allow_slow_non_contiguous=True).then_inc(const_in, 16)
                sp.dma_start(wo_f[:, :, :], w_out_t.rearrange("(a p) n -> p a n", p=P)).then_inc(const_in, 16)
                for s in range(XS):
                    sp.sem_inc(out_st[s], 16)
                with sp.Fori(0, NB) as b:
                    for hp in range(HP):
                        t = b * HP + hp
                        if hp >= 2:
                            sp.wait_ge(freed, done2(b, ("ro", hp - 2, RO - 1)))
                        else:
                            sp.wait_ge(freed, b * NF2 + (BANKS + 1 + pos2["ro", hp + 2, RO - 1]))
                        sp.dma_start(q2[:, hp % 2, :, :, :, :].rearrange("p l g x y -> p (l g x y)"),
                                     q_dram[t].rearrange("h d l g n -> (h d) (l g n)")).then_inc(q_in[hp % 2], 16)
                        sp.wait_ge(cb_lo_done, t + 1)
                        sp.dma_start(c_f[:, :], c_dram[t]).then_inc(c_in, 16)
                        for c in range(YC):
                            sp.wait_ge(yb_lo_done, t * YC + (c + 1))
                            sp.dma_start(y_f[:, c, :, :].rearrange("p x e -> p (x e)"),
                                         y_dram[t].rearrange("g y h x e -> (g y h) (x e)")
                                         [:, c * XY * DK:(c + 1) * XY * DK]).then_inc(y_in[c], 16)
                    for u in range(PR):
                        m, nn = u % CC, u // CC
                        sp.wait_ge(out_st[u % XS], (b * (PR // XS) + (u // XS + 1)) * 16)
                        sp.dma_start(x_res[:, u % XS, :], x_chunks[b, m][:, nn * BANK:(nn + 1) * BANK]
                                     ).then_inc(x_in[u % XS], 16)
                for s in range(XS):
                    sp.wait_ge(out_st[s], 16 * (NB * PR // XS + 1))

            @block.tensor
            def _(pe):
                pe.wait_ge(stat, 1)
                pe.matmul(small_ps[:, 0:2 * DK], ones[:, :], st[:, :, :].rearrange("p s e -> p (s e)"),
                          start=True, stop=True).then_inc(stat_ps, 1)
                pe.wait_ge(stat, NSTAT)
                with pe.Fori(0, NB) as b:
                    for n, (kind, hp, i) in enumerate(fills2):
                        t = b * HP + hp
                        r = n % BANKS
                        pe.wait_ge(freed, b * NF2 + (NF2 + n + 1))
                        if kind == "sy":
                            if i == 0:
                                pe.wait_ge(q_in[hp % 2], (b * 2 + (hp // 2 + 1)) * 16)
                            for j in range(8):
                                y = 8 * i + j
                                for k, (a, m) in enumerate(TERMS):
                                    mm = pe.matmul(bank[:, r, j * 64:j * 64 + 64],
                                                   (rc_hi, rc_lo)[a][:, 2 * (W - 1 - y):2 * (W - 1 - y) + P],
                                                   q2[:, hp % 2, m, y // HALF, :, y % HALF],
                                                   start=k == 0, stop=k == 2)
                        elif kind == "ro":
                            if i == 0:
                                pe.wait_ge(cb_lo_done, t + 2)
                                pe.wait_ge(freed, done2(b, ("sy", hp, SY - 1)))
                            if i % 2 == 0:
                                pe.wait_ge(yb_lo_done, t * YC + (YC + i // 2 + 1))
                            for k, (a, m) in enumerate(TERMS):
                                pe.matmul(bank[:, r, :], (cb_hi, cb_lo)[a][:, hp % 2, :, :].rearrange("p g e -> p (g e)"),
                                          q2[:, hp % 2, m, :, 8 * i:8 * i + 8, :].rearrange("p g x y -> p x g y"),
                                          start=k == 0, stop=False, skip_group_check=True)
                            for j in range(8):
                                xx = 8 * i + j
                                for k, (a, m) in enumerate(TERMS):
                                    mm = pe.matmul(bank[:, r, j * 64:j * 64 + 64],
                                                   (yb_hi, yb_lo)[a][:, xx, :, :].rearrange("p g e -> p (g e)"),
                                                   (sy_hi, sy_lo)[m][:, hp % 2, xx, :],
                                                   start=False, stop=(j == 7 and k == 2), skip_group_check=True)
                        else:
                            if i == 0:
                                pe.wait_ge(freed, done2(b, ("ro", HP - 1, RO - 1)))
                            m, nn = i % CC, i // CC
                            for h in range(HP):
                                for k, (a, mo) in enumerate(TERMS):
                                    mm = pe.matmul(bank[:, r, :], (wo_hi, wo_lo)[a][:, h, m * P:m * P + P],
                                                   (o_hi, o_lo)[mo][:, h, nn * BANK:(nn + 1) * BANK],
                                                   start=(h == 0 and k == 0), stop=(h == HP - 1 and k == 2))
                        mm.then_inc(filled, 1)

            @block.scalar
            def _(act):
                def split_context(t, hp):
                    act.wait_ge(c_in, t * 16 + 16)
                    for g in range(2):
                        s = slice(g * 64, g * 64 + 64)
                        o = act.activation(cb_hi[s, hp % 2, g, :], c_f[s, :], ACT.Copy)
                    o.then_inc(cb_hi_done, 1)

                def split_piece(t, c):
                    act.wait_ge(y_norm, t * (2 * YC) + (2 * c + 2))
                    for g in range(2):
                        o = act.activation(yb_hi[:, c * XY:(c + 1) * XY, g, :], y_f[:, c, :, :], ACT.Copy,
                                           scale=parity[:, g:g + 1])
                    o.then_inc(yb_hi_done, 1)

                def store(b, u):
                    m, nn = u % CC, u // CC
                    act.wait_ge(freed, done2(b, ("pr", 0, u)))
                    act.dma_start(out_chunks[b, m][:, nn * BANK:(nn + 1) * BANK],
                                  x_res[:, u % XS, :]).then_inc(out_st[u % XS], 16)

                act.wait_ge(const_in, 64)
                act.wait_ge(init, 4)
                with act.Fori(0, NB) as b:
                    split_context(b * HP, 0)
                    for n, (kind, hp, i) in enumerate(fills2):
                        t = b * HP + hp
                        if kind == "pr":
                            act.wait_ge(x_in[i % XS], (b * (PR // XS) + (i // XS + 1)) * 16)
                            act.activation(x_res[:, i % XS, :], x_res[:, i % XS, :], ACT.Identity,
                                           bias=bias[:, i % CC:i % CC + 1]).then_inc(hi_done, 1)
                            if i > 0:
                                store(b, i - 1)
                            continue
                        act.wait_ge(filled, b * NF2 + (n + 1))
                        src = bank[:, n % BANKS, :]
                        if kind == "sy":
                            act.activation(sy_hi[:, hp % 2, :, 8 * i:8 * i + 8],
                                           src.rearrange("p (y x) -> p x y", y=8), ACT.Copy).then_inc(hi_done, 1)
                            if hp == 0 and i % 2 == 1:
                                split_piece(t, i // 2)
                        else:
                            act.activation(o_hi[:, hp, i * BANK:(i + 1) * BANK], src, ACT.Copy).then_inc(hi_done, 1)
                            if hp + 1 < HP:
                                if i == 0:
                                    split_context(t + 1, hp + 1)
                                if i % 2 == 1:
                                    split_piece(t + 1, i // 2)
                    store(b, PR - 1)

            @block.vector
            def _(dve):
                for tile in (cb_hi, cb_lo):
                    dve.memset(tile[0:64, :, 1, :], 0.0).then_inc(init, 1)
                    dve.memset(tile[64:128, :, 0, :], 0.0).then_inc(init, 1)
                dve.sem_inc(freed, BANKS + NF2)
                dve.sem_inc(yb_lo_done, YC)
                dve.sem_inc(cb_lo_done, 1)
                dve.tensor_reduce(st[:, :, :], acc[:, :, :].rearrange("p s (g e) -> p s e g", e=DK), AX.X,
                                  ALU.add).then_inc(stat, 1)
                dve.wait_ge(const_in, 64)
                dve.wait_ge(stat_ps, 1)
                dve.tensor_scalar(mean[:, :], small_ps[:, 0:DK], 1.0 / N_BN, None, ALU.mult).then_inc(stat, 1)
                dve.tensor_scalar(var[:, :], small_ps[:, DK:2 * DK], 1.0 / N_BN, None, ALU.mult).then_inc(stat, 1)
                dve.wait_ge(stat, 3)
                dve.tensor_tensor(y_mul[:, :], mean[:, :], mean[:, :], ALU.mult).then_inc(stat, 1)
                dve.wait_ge(stat, 4)
                dve.tensor_tensor(var[:, :], var[:, :], y_mul[:, :], ALU.subtract).then_inc(stat, 1)
                dve.wait_ge(stat, 5)
                dve.tensor_scalar(var[:, :], var[:, :], factors[:, 1:2], factors[:, 1:2],
                                  ALU.mult, ALU.mult).then_inc(stat, 1)
                dve.wait_ge(stat, 6)
                dve.tensor_scalar(var[:, :], var[:, :], 0.0, BN_EPS, ALU.max, ALU.add).then_inc(stat, 1)
                dve.wait_ge(root, 1)
                dve.tensor_tensor(y_mul[:, :], var[:, :], gam[:, :], ALU.mult).then_inc(stat, 1)
                dve.wait_ge(stat, 8)
                dve.tensor_scalar(y_mul[:, :], y_mul[:, :], factors[:, 1:2], None, ALU.mult).then_inc(stat, 1)
                dve.wait_ge(stat, 9)
                dve.tensor_tensor(mean[:, :], mean[:, :], y_mul[:, :], ALU.mult).then_inc(stat, 1)
                dve.wait_ge(stat, 10)
                dve.tensor_tensor(y_add[:, :], bet[:, :], mean[:, :], ALU.subtract).then_inc(stat, 1)
                dve.tensor_scalar(wo_f[:, :, :], wo_f[:, :, :], inv_all[:, 3:4], None, ALU.mult).then_inc(init, 1)
                dve.wait_ge(init, 5)
                dve.tensor_copy(wo_hi[:, :, :], wo_f[:, :, :]).then_inc(init, 1)
                dve.wait_ge(init, 6)
                dve.tensor_tensor(wo_lo[:, :, :], wo_f[:, :, :], wo_hi[:, :, :], ALU.subtract).then_inc(stat, 1)

                def split_context(t, hp):
                    dve.wait_ge(cb_hi_done, t + 1)
                    for g in range(2):
                        s = slice(g * 64, g * 64 + 64)
                        o = dve.tensor_tensor(cb_lo[s, hp % 2, g, :], c_f[s, :], cb_hi[s, hp % 2, g, :], ALU.subtract)
                    o.then_inc(cb_lo_done, 1)

                def split_piece(t, c):
                    dve.wait_ge(yb_hi_done, t * YC + (c + 1))
                    for g in range(2):
                        s = slice(c * XY, (c + 1) * XY)
                        o = dve.scalar_tensor_tensor(yb_lo[:, s, g, :], y_f[:, c, :, :], parity[:, g:g + 1],
                                                     yb_hi[:, s, g, :], ALU.mult, ALU.subtract)
                    o.then_inc(yb_lo_done, 1)

                with dve.Fori(0, NB) as b:
                    split_context(b * HP, 0)
                    for n, (kind, hp, i) in enumerate(fills2):
                        t = b * HP + hp
                        dve.wait_ge(hi_done, b * NF2 + (n + 1))
                        src = bank[:, n % BANKS, :]
                        if kind == "sy":
                            s = slice(8 * i, 8 * i + 8)
                            dve.tensor_tensor(sy_lo[:, hp % 2, :, s], src.rearrange("p (y x) -> p x y", y=8),
                                              sy_hi[:, hp % 2, :, s], ALU.subtract).then_inc(freed, 1)
                            if hp == 0 and i % 2 == 1:
                                split_piece(t, i // 2)
                        elif kind == "ro":
                            s = slice(i * BANK, (i + 1) * BANK)
                            dve.tensor_tensor(o_lo[:, hp, s], src, o_hi[:, hp, s], ALU.subtract).then_inc(freed, 1)
                            if hp + 1 < HP:
                                if i == 0:
                                    split_context(t + 1, hp + 1)
                                if i % 2 == 1:
                                    split_piece(t + 1, i // 2)
                        else:
                            dve.wait_ge(filled, b * NF2 + (n + 1))
                            dve.scalar_tensor_tensor(x_res[:, i % XS, :], src, factors[:, 2:3],
                                                     x_res[:, i % XS, :], ALU.mult, ALU.add).then_inc(freed, 1)

            @block.gpsimd
            def _(pool):
                pool.wait_ge(stat, 7)
                pool.tensor_tensor(var[:, :], var[:, :], minus_half[:, :], ALU.pow).then_inc(root, 1)
                pool.wait_ge(stat, 11)
                with pool.Fori(0, NT) as t:
                    for c in range(YC):
                        yy = y_f[:, c, :, :]
                        pool.wait_ge(y_in[c], t * 16 + 16)
                        pool.tensor_tensor(yy, yy, y_mul[:, :].unsqueeze(1).to_broadcast([P, XY, DK]),
                                           ALU.mult).then_inc(y_norm, 1)
                        pool.wait_ge(y_norm, t * (2 * YC) + (2 * c + 1))
                        pool.tensor_tensor(yy, yy, y_add[:, :].unsqueeze(1).to_broadcast([P, XY, DK]),
                                           ALU.add).then_inc(y_norm, 1)


def kernel(x, L0_conv_w_qkv, L0_conv_w_out, L0_conv_b_out, L0_conv_rel_rows, L0_conv_rel_columns,
           L0_conv_bn_gamma, L0_conv_bn_beta):
    import numpy as np
    import concourse.bacc as bacc
    from concourse.bass_utils import run_bass_kernel_spmd

    nc = bacc.Bacc("TRN2", target_bir_lowering=False, num_devices=1)
    arrays = {
        "x": np.ascontiguousarray(x),
        "w_qkv_t": np.ascontiguousarray(np.asarray(L0_conv_w_qkv).T),
        "w_out_t": np.ascontiguousarray(np.asarray(L0_conv_w_out).T),
        "b_out": np.ascontiguousarray(L0_conv_b_out),
        "rel_rows_t": np.ascontiguousarray(np.asarray(L0_conv_rel_rows).T),
        "rel_cols_t": np.ascontiguousarray(np.asarray(L0_conv_rel_columns).T),
        "gamma": np.ascontiguousarray(L0_conv_bn_gamma),
        "beta": np.ascontiguousarray(L0_conv_bn_beta),
        "ident_in": np.eye(128, dtype=np.float32),
        "group_in": np.kron(np.eye(16, dtype=np.float32), np.full((8, 8), 0.125, np.float32)),
        "parity_in": np.eye(2, dtype=np.float32)[np.arange(128) % 2],
    }
    args = [nc.dram_tensor(n, a.shape, mybir.dt.from_np(a.dtype), kind="ExternalInput").ap()
            for n, a in arrays.items()]
    out = nc.dram_tensor("out", arrays["x"].shape, F32, kind="ExternalOutput").ap()
    attention_kernel(nc, *args, out)
    r = run_bass_kernel_spmd(nc, [arrays], core_ids=[0])
    return r.results[0]["out"]
```

```python
from contextlib import ExitStack

import concourse.bass as bass
from concourse import mybir

F32 = mybir.dt.float32
F16 = mybir.dt.float16
ALU = mybir.AluOpType
ACT = mybir.ActivationFunctionType
AX = mybir.AxisListType

P = 128
GN_EPS = 1e-5
BN_EPS = 1e-5
TINY = 1e-30
BANKS = 5
BANK = 512
YST = 2
YSQ = 2


def attention_kernel(nc, x, w_qkv_t, w_out_t, b_out, rel_rows_t, rel_cols_t, gamma, beta,
                     ident_in, group_in, parity_in, out):
    NB, C, H, W = x.shape
    CC = C // P
    DK = rel_rows_t.shape[0]
    HID = w_out_t.shape[0]
    HP = HID // P
    PIX = H * W
    HALF = W // 2
    NT = NB * HP
    NREL = 2 * W - 1
    assert DK == 64 and H == 64 and W == 64 and CC == 2 and HP == 4
    x_chunks = x.rearrange("b (c p) h w -> b c p (h w)", p=P)
    out_chunks = out.rearrange("b (c p) h w -> b c p (h w)", p=P)
    N_BN = float(NB * (HID // DK) * PIX)

    q_dram = nc.dram_tensor("q_scratch", (NT, 2, DK, 2, 2, H * HALF), F16, kind="Internal").ap()
    y_dram = nc.dram_tensor("y_scratch", (NT, 2, HALF, 2, H, DK), F32, kind="Internal").ap()
    c_dram = nc.dram_tensor("ctx_scratch", (NT, P, DK), F32, kind="Internal").ap()

    TERMS = ((0, 0), (0, 1), (1, 0))

    KV, Q, SX, YH = 16, 8, 8, 8

    def turn_of(first=False, final=False):
        order = [("kv", 0, i) for i in range(KV)] if first else []
        for hp in range(HP):
            for i in range(Q):
                order.append(("q", hp, i))
                if not (first and hp == 0):
                    order.append(("yh", hp - 1, i))
            if final and hp == HP - 1:
                order += [("sx", hp, i) for i in range(SX)] + [("yh", hp, i) for i in range(YH)]
            elif hp == HP - 1 or (first and hp == 0):
                order += [("sx", hp, i) for i in range(SX)] + [("kv", hp + 1, i) for i in range(KV)]
            else:
                for i in range(SX):
                    order += [("sx", hp, i), ("kv", hp + 1, i)]
                order += [("kv", hp + 1, i) for i in range(SX, KV)]
        return order

    first_turn, loop_turn, final_turn = turn_of(first=True), turn_of(), turn_of(final=True)
    NF = len(loop_turn)
    SHIFT = len(first_turn) - NF
    assert NF % BANKS == 0

    def at(b, key):
        if isinstance(b, int) and b == 0:
            return first_turn.index(key)
        kind, hp, i = key
        order = final_turn if isinstance(b, int) and b == NB - 1 else loop_turn
        if hp < 0 and kind != "yh":
            return b * NF + (SHIFT + loop_turn.index((kind, HP + hp, i)) - NF)
        return b * NF + (SHIFT + order.index(key))

    with ExitStack() as top:
        def sb(name, shape, dt, c=top):
            return c.enter_context(nc.sbuf_tensor(name, list(shape), dt))

        def ps(name, shape, c=top):
            return c.enter_context(nc.psum_tensor(name, list(shape), F32))

        def sem(name, c=top):
            return c.enter_context(nc.semaphore(name))

        bank = ps("bank", [P, BANKS, BANK])
        ctx_ps = ps("ctx_ps", [P, BANK])
        small_ps = ps("small_ps", [P, BANK])
        gn_ps = ps("gn_ps", [P, BANK])

        scale_all = sb("scale_all", [P, 4], F32)
        inv_all = sb("inv_all", [P, 4], F32)
        factors = sb("factors", [P, 4], F32)
        rc_hi = sb("rc_hi", [P, 2 * P], F16)
        rc_lo = sb("rc_lo", [P, 2 * P], F16)
        ones = sb("ones", [P, P], F32)
        parity = sb("parity", [P, 2], F32)
        minus_half = sb("minus_half", [P, DK], F32)
        acc = sb("acc", [P, 2, BANK], F32)

        p1 = ExitStack()
        w_hi = sb("w_hi", [P, CC, 3 * HID], F16, p1)
        w_lo = sb("w_lo", [P, CC, 3 * HID], F16, p1)
        rr_hi = sb("rr_hi", [P, 2 * P], F16, p1)
        rr_lo = sb("rr_lo", [P, 2 * P], F16, p1)
        ident = sb("ident", [P, P], F32, p1)
        group = sb("group", [P, P], F32, p1)

        x_f = sb("x_f", [P, CC, PIX], F32, p1)
        x_in = sem("x_in", p1)

        with ExitStack() as st, nc.Block() as block:
            w_f = sb("w_f", [P, CC, 3 * HID], F32, st)
            rr_f = sb("rr_f", [P, 2 * P], F32, st)
            rc_f = sb("rc_f", [P, 2 * P], F32, st)
            wo_f = sb("wo_f", [P, HP, C], F32, st)
            mx = sb("mx", [P, 4], F32, st)
            rel_in = sb("rel_in", [P, 2, NREL], F32, st)
            s_zero = sem("s_zero", st)
            s_ld = sem("s_ld", st)
            s_mx = sem("s_mx", st)
            s_all = sem("s_all", st)
            s_sc = sem("s_sc", st)
            s_hi = sem("s_hi", st)

            @block.sync
            def _(sp):
                sp.dma_start(w_f[:, :, :], w_qkv_t.rearrange("(a p) n -> p a n", p=P)).then_inc(s_ld, 16)
                sp.dma_start(wo_f[:, :, :], w_out_t.rearrange("(a p) n -> p a n", p=P)).then_inc(s_ld, 16)
                sp.dma_start(ident[:, :], ident_in[:, :]).then_inc(s_ld, 16)
                sp.dma_start(group[:, :], group_in[:, :]).then_inc(s_ld, 16)
                sp.dma_start(parity[:, :], parity_in[:, :]).then_inc(s_ld, 16)
                for g in range(2):
                    sp.dma_start(rel_in[g * 64:g * 64 + 64, 0, :], rel_rows_t[:, :]).then_inc(s_ld, 16)
                    sp.dma_start(rel_in[g * 64:g * 64 + 64, 1, :], rel_cols_t[:, :]).then_inc(s_ld, 16)
                for c in range(CC):
                    sp.dma_start(x_f[:, c, :], x_chunks[0, c]).then_inc(x_in, 16)
                sp.wait_ge(s_ld, 144)

            @block.gpsimd
            def _(pool):
                pool.wait_ge(s_mx, 4)
                pool.partition_all_reduce(scale_all[:, :], mx[:, :], P, bass.bass_isa.ReduceOp.max).then_inc(s_all, 1)
                pool.memset(minus_half[:, :], -0.5).then_inc(s_all, 1)

            @block.vector
            def _(dve):
                dve.memset(rr_f[:, :], 0.0).then_inc(s_zero, 1)
                dve.memset(rc_f[:, :], 0.0).then_inc(s_zero, 1)
                dve.memset(ones[:, :], 1.0)
                dve.wait_ge(s_ld, 144)
                dve.wait_ge(s_zero, 2)
                for g in range(2):
                    s = slice(g * 64, g * 64 + 64)
                    dve.tensor_copy(rr_f[s, g:2 * NREL:2], rel_in[s, 0, :]).then_inc(s_zero, 1)
                    dve.tensor_copy(rc_f[s, g:2 * NREL:2], rel_in[s, 1, :]).then_inc(s_zero, 1)
                dve.wait_ge(s_zero, 6)
                for n, t in enumerate((w_f[:, :, :], rr_f[:, :], rc_f[:, :], wo_f[:, :, :])):
                    axis = AX.XY if n in (0, 3) else AX.X
                    dve.tensor_reduce(mx[:, n:n + 1], t, axis, ALU.max,
                                      apply_absolute_value=True).then_inc(s_mx, 1)
                dve.wait_ge(s_all, 1)
                dve.tensor_scalar(scale_all[:, :], scale_all[:, :], TINY, None, ALU.max).then_inc(s_sc, 1)
                dve.wait_ge(s_sc, 1)
                dve.reciprocal(inv_all[:, :], scale_all[:, :]).then_inc(s_sc, 1)
                dve.tensor_tensor(factors[:, 1:2], scale_all[:, 0:1], scale_all[:, 0:1], ALU.mult).then_inc(s_sc, 1)
                dve.tensor_tensor(factors[:, 2:3], scale_all[:, 0:1], scale_all[:, 2:3], ALU.mult).then_inc(s_sc, 1)
                dve.wait_ge(s_sc, 4)
                dve.tensor_tensor(factors[:, 0:1], scale_all[:, 0:1], inv_all[:, 2:3], ALU.mult).then_inc(s_sc, 1)
                dve.tensor_tensor(factors[:, 1:2], factors[:, 1:2], scale_all[:, 1:2], ALU.mult).then_inc(s_sc, 1)
                dve.tensor_tensor(factors[:, 2:3], factors[:, 2:3], scale_all[:, 3:4], ALU.mult).then_inc(s_sc, 1)
                for k, (src, hi, lo) in enumerate(((w_f[:, :, :], w_hi[:, :, :], w_lo[:, :, :]),
                                                   (rr_f[:, :], rr_hi[:, :], rr_lo[:, :]),
                                                   (rc_f[:, :], rc_hi[:, :], rc_lo[:, :]))):
                    dve.wait_ge(s_hi, k + 1)
                    dve.scalar_tensor_tensor(lo, src, inv_all[:, k:k + 1], hi,
                                             ALU.mult, ALU.subtract).then_inc(s_sc, 1)
                dve.wait_ge(s_sc, 10)

            @block.scalar
            def _(act):
                act.wait_ge(s_sc, 2)
                for k, (src, hi) in enumerate(((w_f[:, :, :], w_hi[:, :, :]), (rr_f[:, :], rr_hi[:, :]),
                                               (rc_f[:, :], rc_hi[:, :]))):
                    act.activation(hi, src, ACT.Copy, scale=inv_all[:, k:k + 1]).then_inc(s_hi, 1)

        with p1, nc.Block() as block:
            x_hi = sb("x_hi", [P, CC, PIX], F16, p1)
            x_lo = sb("x_lo", [P, CC, PIX], F16, p1)
            k_f = sb("k_f", [P, HALF, P], F32, p1)
            p_hi = sb("p_hi", [P, HALF, P], F16, p1)
            p_lo = sb("p_lo", [P, HALF, P], F16, p1)
            VW = P + 2
            v_hi = sb("v_hi", [P, 2, HALF, VW], F16, p1)
            v_lo = sb("v_lo", [P, 2, HALF, VW], F16, p1)
            q_hi = sb("q_hi", [P, 2, H, HALF], F16, p1)
            q_lo = sb("q_lo", [P, 2, H, HALF], F16, p1)
            sx_hi = sb("sx_hi", [P, 2 * HALF, 2, H], F16, p1)
            sx_lo = sb("sx_lo", [P, 2 * HALF, 2, H], F16, p1)
            yst = sb("yst", [P, YST, BANK], F32, p1)
            ysq = sb("ysq", [P, YSQ, BANK], F32, p1)
            kmax_halves = sb("kmax_halves", [P, 2, P], F32, p1)
            kmax = sb("kmax", [P, P], F32, p1)
            diag = sb("diag", [P, P], F32, p1)
            negmax = sb("negmax", [P, P], F32, p1)
            colmax = sb("colmax", [P, 1], F32, p1)
            cden = sb("cden", [P, 1], F32, p1)
            cst = sb("cst", [P, DK], F32, p1)
            bn6 = sb("bn6", [P, CC, 8, 6], F32, p1)
            mv = sb("mv", [P, CC, 2], F32, p1)
            spare = sb("spare", [P, 2], F32, p1)
            gs = sb("gs", [P, CC, 2], F32, p1)
            rstd = sb("rstd", [P, CC], F32, p1)
            nbias = sb("nbias", [P, CC], F32, p1)

            filled = sem("filled", p1)
            hi_done = sem("hi_done", p1)
            freed = sem("freed", p1)
            bn_done = sem("bn_done", p1)
            gn_sum = sem("gn_sum", p1)
            gn_root = sem("gn_root", p1)
            x_norm = sem("x_norm", p1)
            x_hi_a = sem("x_hi_a", p1)
            x_hi_b = sem("x_hi_b", p1)
            x_lo_done = sem("x_lo_done", p1)
            kmax_done = sem("kmax_done", p1)
            small = sem("small", p1)
            max_done = sem("max_done", p1)
            shifted = sem("shifted", p1)
            exp_done = sem("exp_done", p1)
            p_hi_done = sem("p_hi_done", p1)
            p_lo_a = sem("p_lo_a", p1)
            p_lo_b = sem("p_lo_b", p1)
            ctx_done = sem("ctx_done", p1)
            ctx_out = sem("ctx_out", p1)
            ctx_st = sem("ctx_st", p1)
            q_st = sem("q_st", p1)
            y_st = [sem(f"y_st{s}", p1) for s in range(YST)]
            sums = sem("sums", p1)
            squares = sem("squares", p1)
            init = sem("init", p1)

            NXC = 4
            XC = PIX // NXC
            XPOOL = 2
            NBN = 16 + 1 + 2 + 2 + 1 + 4 + 2

            def evacuated(b, key):
                return at(b, key) + (BANKS + 1)

            def bank_of(order, n):
                return (n if order is first_turn else n + SHIFT) % BANKS

            def chain(order, n):
                start = [(h, n - order.index(("q", h, 0))) for h in range(HP)]
                return [(h, j) for h, j in start if 0 <= j < 16]

            def turns(eng, turn):
                turn(0, first_turn)
                with eng.Fori(1, NB - 1) as b:
                    turn(b, loop_turn)
                turn(NB - 1, final_turn)

            xh_kv = [t[:, :, :].rearrange("p c (k y) -> p c y k", y=HALF) for t in (x_hi, x_lo)]
            xh_q = [t[:, :, :].rearrange("p c (x g y) -> p c g x y", g=2, y=HALF) for t in (x_hi, x_lo)]
            w_kv = [t[:, :, HID:3 * HID].rearrange("p c (t n) -> p c t n", t=2) for t in (w_hi, w_lo)]
            @block.sync
            def _(sp):
                def load_x(index):
                    for c in range(CC):
                        sp.dma_start(x_f[:, c, :], x_chunks[index, c]).then_inc(x_in, 16)

                sp.sem_inc(q_st, 64)
                sp.sem_inc(ctx_st, 16)
                for s in range(YST):
                    sp.sem_inc(y_st[s], 32)
                def store_y(b, hp, i):
                    sp.wait_ge(freed, evacuated(b, ("yh", hp, i)))
                    for g in range(2):
                        sp.dma_start(y_dram[b * HP + hp, g, 4 * i:4 * i + 4].rearrange("y h x e -> x (y h) e"),
                                     yst[g * 64:g * 64 + 64, i % YST, :].rearrange("p (y e) -> p y e", e=DK)
                                     ).then_inc(y_st[i % YST], 16)

                def store_context(t):
                    sp.wait_ge(ctx_out, t * 3 + 4)
                    sp.dma_start(c_dram[t], cst[:, :]).then_inc(ctx_st, 16)

                def turn(b, order):
                    if order is not final_turn:
                        sp.wait_ge(x_lo_done, (b + 1) * (CC * NXC))
                        load_x(b + 1)
                    for hp in range(HP):
                        before = order is not first_turn or hp > 0
                        if before:
                            for i in range(4):
                                store_y(b, hp - 1, i)
                            store_context(b * HP + (hp - 1))
                            for i in range(4, YH - 1):
                                store_y(b, hp - 1, i)
                        sp.wait_ge(freed, evacuated(b, ("q", hp, Q - 1)))
                        for part, src in enumerate((q_hi, q_lo)):
                            for g in range(2):
                                sp.dma_start(q_dram[b * HP + hp].rearrange("h d l g n -> l g d h n")[part, g],
                                             src[g * 64:g * 64 + 64, :, :, :].rearrange("p h x y -> p h (x y)")
                                             ).then_inc(q_st, 16)
                        if before:
                            store_y(b, hp - 1, YH - 1)
                    if order is final_turn:
                        for i in range(YH):
                            store_y(b, HP - 1, i)
                        store_context(b * HP + (HP - 1))

                turns(sp, turn)
                sp.wait_ge(q_st, 64 * (NT + 1))
                sp.wait_ge(ctx_st, 16 * (NT + 1))
                for s in range(YST):
                    sp.wait_ge(y_st[s], 32 * (NT * YH // YST + 1))
                sp.wait_ge(x_in, 16 * CC * NB)

            @block.tensor
            def _(pe):
                def pairs(outs, lhs, rhs, first, last, **kw):
                    for n, (a, m) in enumerate(TERMS):
                        mm = pe.matmul(outs, lhs[a], rhs[m], start=first and n == 0,
                                       stop=last and n == 2, **kw)
                    return mm

                def gn_groups(nth):
                    pe.wait_ge(bn_done, nth * NBN + 21)
                    pe.matmul(gn_ps[:, 0:4], group[:, :], mv[:, :, :].rearrange("p c k -> p (c k)"),
                              start=True, stop=True).then_inc(gn_sum, 1)

                pe.sem_inc(ctx_done, 1)
                gn_groups(0)
                def context_piece(b, hp, piece):
                    t = b * HP + hp
                    if piece == 0:
                        pe.wait_ge(p_lo_a, t * 2 + 2)
                        pe.wait_ge(p_lo_b, t * 2 + 2)
                        pe.wait_ge(ctx_out, t * 3 + 1)
                    for y2 in range(4 * piece, 4 * piece + 4):
                        for k, (a, m) in enumerate(TERMS):
                            mm = pe.matmul(ctx_ps[:, 0:VW], (p_hi, p_lo)[a][:, y2, :],
                                           (v_hi, v_lo)[m][:, hp % 2, y2, :],
                                           start=(y2 == 0 and k == 0), stop=(y2 == HALF - 1 and k == 2))
                    if piece == 7:
                        mm.then_inc(ctx_done, 1)

                def turn(b, order):
                    for n, (kind, hp, i) in enumerate(order):
                        N = at(b, (kind, hp, i))
                        r = bank_of(order, n)
                        pe.wait_ge(freed, N + 1)
                        if kind == "kv":
                            if hp % HP == 0 and i == 0:
                                image = b + hp // HP
                                pe.wait_ge(x_lo_done, (image + 1) * (CC * NXC))
                            for j in range(2):
                                y2, c0 = 2 * i + j, (hp % HP) * P
                                for c in range(CC):
                                    mm = pairs(bank[:, r, j * 256:j * 256 + 256],
                                               [s[:, c, y2] for s in xh_kv],
                                               [s[:, c, :, c0:c0 + P] for s in w_kv],
                                               c == 0, c == CC - 1)
                        elif kind == "q":
                            x0, h2 = (i // 2) * 16, i % 2
                            for c in range(CC):
                                for k, (a, m) in enumerate(TERMS):
                                    for g in range(2):
                                        ww = (w_hi, w_lo)[a][:, c, hp * P + h2 * 64:hp * P + h2 * 64 + 64]
                                        mm = pe.matmul(bank[g * 64:g * 64 + 64, r, :], ww,
                                                       xh_q[m][:, c, g, x0:x0 + 16, :],
                                                       start=(c == 0 and k == 0), stop=(c == CC - 1 and k == 2))
                        elif kind == "sx":
                            if i % 2 == 0:
                                pe.wait_ge(freed, evacuated(b, ("q", hp, i + 1)))
                            for j in range(8):
                                xx = 8 * i + j
                                mm = pairs(bank[:, r, j * 64:j * 64 + 64],
                                           [s[:, 2 * (H - 1 - xx):2 * (H - 1 - xx) + P] for s in (rr_hi, rr_lo)],
                                           [s[:, :, xx, :] for s in (q_hi, q_lo)], True, True)
                        else:
                            if i == 0:
                                pe.wait_ge(freed, evacuated(b, ("sx", hp, SX - 1)))
                            for j in range(4):
                                y2 = 4 * i + j
                                for h2 in range(2):
                                    mm = pairs(bank[:, r, (2 * j + h2) * 64:(2 * j + h2) * 64 + 64],
                                               [s[:, h2 * HALF + y2, :, :].rearrange("p g x -> p (g x)") for s in (sx_hi, sx_lo)],
                                               [s[:, hp % 2, y2, h2 * 64:h2 * 64 + 64] for s in (v_hi, v_lo)],
                                               True, True)
                        mm.then_inc(filled, 1)
                        for h, j in chain(order, n):
                            t = b * HP + h
                            if j < 8 and not (order is first_turn and h == 0):
                                context_piece(b, h - 1, j)
                            if j == 1:
                                pe.wait_ge(kmax_done, t * 3 + 3)
                                pe.transpose(small_ps[:, 0:P], kmax[:, :], ident[:, :]).then_inc(small, 1)
                            if j == 4:
                                pe.wait_ge(max_done, t * 3 + 2)
                                pe.matmul(small_ps[:, P:2 * P], ones[:, :], diag[:, :],
                                          start=True, stop=True).then_inc(small, 1)
                            if (h, j) == (2, 4) and order is not final_turn:
                                gn_groups(b + 1)
                        if (kind, hp) == ("yh", HP - 1):
                            context_piece(b, hp, i)

                turns(pe, turn)

            @block.scalar
            def _(act):
                def split_x(nth, piece):
                    act.wait_ge(x_norm, nth * 8 + piece * CC + 1)
                    s = slice(piece * XC, piece * XC + XC)
                    act.activation(x_hi[:, 0, s], x_f[:, 0, s], ACT.Copy).then_inc(x_hi_a, 1)

                for piece in range(NXC):
                    split_x(0, piece)
                act.wait_ge(init, 4)
                def turn(b, order):
                    for n, (kind, hp, i) in enumerate(order):
                        t = b * HP + hp
                        r = bank_of(order, n)
                        src = bank[:, r, :]
                        if kind == "kv" and i % 4 == 0 and not (order is first_turn and hp == 0):
                            act.wait_ge((p_lo_a, p_lo_b)[i // 8], t * 2 + (i // 4 % 2 - 1))
                        if kind == "q" and i == 0:
                            act.wait_ge(q_st, t * 64 + 64)
                        if kind == "yh" and hp == HP - 1 and i >= YSQ:
                            act.wait_ge(squares, i - YSQ + 1)
                        elif kind == "yh":
                            act.wait_ge(sums, (t * YH + i) * 2 + 4)
                        act.wait_ge(filled, at(b, (kind, hp, i)) + 1)
                        if kind == "kv":
                            v = src.rearrange("p (j t n) -> p j t n", j=2, t=2)
                            act.activation(k_f[:, 2 * i:2 * i + 2, :], v[:, :, 0, :], ACT.Copy)
                            act.activation(v_hi[:, hp % 2, 2 * i:2 * i + 2, 0:P], v[:, :, 1, :],
                                           ACT.Copy).then_inc(hi_done, 1)
                        elif kind == "q":
                            x0, h2 = (i // 2) * 16, i % 2
                            act.activation(q_hi[:, h2, x0:x0 + 16, :].rearrange("p x y -> p (x y)"), src,
                                           ACT.Copy).then_inc(hi_done, 1)
                        elif kind == "sx":
                            for g in range(2):
                                o = act.activation(sx_hi[:, :, g, 8 * i:8 * i + 8],
                                                   src.rearrange("p (x h) -> p h x", x=8),
                                                   ACT.Copy, scale=parity[:, g:g + 1])
                            o.then_inc(hi_done, 1)
                        else:
                            act.activation(ysq[:, i % YSQ, :], src, ACT.Square).then_inc(hi_done, 1)
                        for h, j in chain(order, n):
                            c = (b * HP + h) * 4
                            if 7 <= j < 11:
                                act.wait_ge(shifted, c + (j - 6))
                                kk = k_f[:, 8 * (j - 7):8 * (j - 7) + 8, :]
                                act.activation(kk, kk, ACT.Exp, scale=scale_all[:, 0:1]).then_inc(exp_done, 1)
                            if 9 <= j < 13:
                                act.wait_ge(exp_done, c + (j - 8))
                                act.wait_ge(ctx_done, b * HP + (h + 1))
                                s = slice(8 * (j - 9), 8 * (j - 9) + 8)
                                act.activation(p_hi[:, s, :], k_f[:, s, :], ACT.Copy).then_inc(p_hi_done, 1)
                        if kind == "q" and hp == HP - 1 and i % 2 == 1 and order is not final_turn:
                            split_x(b + 1, i // 2)

                turns(act, turn)

            def context_out(dve, t):
                dve.wait_ge(ctx_done, t + 2)
                dve.wait_ge(ctx_st, t * 16 + 16)
                dve.reciprocal(cden[:, :], ctx_ps[:, P:P + 1]).then_inc(ctx_out, 1)
                dve.wait_ge(ctx_out, t * 3 + 2)
                for g in range(2):
                    s = slice(g * 64, g * 64 + 64)
                    dve.tensor_scalar(cst[s, :], ctx_ps[s, g * 64:g * 64 + 64], cden[s, 0:1], factors[s, 0:1],
                                      ALU.mult, ALU.mult).then_inc(ctx_out, 1)

            @block.vector
            def _(dve):
                dve.memset(v_hi[:, 0, :, P:VW], 1.0).then_inc(init, 1)
                dve.memset(v_hi[:, 1, :, P:VW], 1.0).then_inc(init, 1)
                dve.memset(v_lo[:, 0, :, P:VW], 0.0).then_inc(init, 1)
                dve.memset(v_lo[:, 1, :, P:VW], 0.0).then_inc(init, 1)
                dve.sem_inc(freed, BANKS)
                dve.sem_inc(ctx_out, 1)

                def gn_stats(nth, k):
                    c, j = k // 8, k % 8
                    if k % 8 == 0:
                        dve.wait_ge(x_in, nth * 16 * CC + 16 * CC)
                    dve.bn_stats(bn6[:, c, j, :], x_f[:, c, j * 512:j * 512 + 512]).then_inc(bn_done, 1)

                def gn_channels(nth):
                    base = nth * NBN
                    dve.wait_ge(bn_done, base + 16)
                    dve.memset(spare[:, 0:2], 0.0).then_inc(bn_done, 1)
                    for c in range(CC):
                        dve.bn_aggr(mv[:, c, :], bn6[:, c, :, :].rearrange("p a b -> p (a b)")).then_inc(bn_done, 1)
                    dve.wait_ge(bn_done, base + 19)
                    for c in range(CC):
                        dve.scalar_tensor_tensor(mv[:, c, 1:2], mv[:, c, 0:1], mv[:, c, 0:1], mv[:, c, 1:2],
                                                 ALU.mult, ALU.add).then_inc(bn_done, 1)

                def gn_scale(nth):
                    base = nth * NBN + 21
                    dve.wait_ge(gn_sum, nth + 1)
                    dve.tensor_copy(gs[:, :, :].rearrange("p c k -> p (c k)"), gn_ps[:, 0:4]).then_inc(bn_done, 1)
                    dve.wait_ge(bn_done, base + 1)
                    dve.tensor_tensor(rstd[:, :], gs[:, :, 0], gs[:, :, 0], ALU.mult).then_inc(bn_done, 1)
                    dve.wait_ge(bn_done, base + 2)
                    dve.tensor_tensor(rstd[:, :], gs[:, :, 1], rstd[:, :], ALU.subtract).then_inc(bn_done, 1)
                    dve.wait_ge(bn_done, base + 3)
                    dve.tensor_scalar(rstd[:, :], rstd[:, :], 0.0, None, ALU.max).then_inc(bn_done, 1)
                    dve.wait_ge(bn_done, base + 4)
                    dve.tensor_scalar(rstd[:, :], rstd[:, :], GN_EPS, None, ALU.add).then_inc(bn_done, 1)

                def gn_bias(nth):
                    base = nth * NBN + 21
                    dve.wait_ge(gn_root, nth + 1)
                    dve.tensor_tensor(nbias[:, :], gs[:, :, 0], rstd[:, :], ALU.mult).then_inc(bn_done, 1)
                    dve.wait_ge(bn_done, base + 6)
                    dve.tensor_scalar(nbias[:, :], nbias[:, :], -1.0, None, ALU.mult).then_inc(bn_done, 1)

                def gn_apply(nth, k):
                    c, j = k % CC, k // CC
                    if k == 0:
                        dve.wait_ge(bn_done, nth * NBN + NBN)
                    s = x_f[:, c, j * XC:j * XC + XC]
                    dve.tensor_scalar(s, s, rstd[:, c:c + 1], nbias[:, c:c + 1],
                                      ALU.mult, ALU.add).then_inc(x_norm, 1)

                def split_x(nth, j):
                    s = slice(j * XC, j * XC + XC)
                    dve.wait_ge(x_norm, nth * 8 + (CC * j + 2))
                    dve.tensor_copy(x_hi[:, 1, s], x_f[:, 1, s]).then_inc(x_hi_b, 1)
                    dve.wait_ge(x_hi_a, nth * NXC + (j + 1))
                    dve.tensor_tensor(x_lo[:, 0, s], x_f[:, 0, s], x_hi[:, 0, s], ALU.subtract).then_inc(x_lo_done, 1)
                    if j >= XPOOL:
                        dve.wait_ge(x_hi_b, nth * NXC + (j + 1))
                        dve.tensor_tensor(x_lo[:, 1, s], x_f[:, 1, s], x_hi[:, 1, s], ALU.subtract).then_inc(x_lo_done, 1)

                for k in range(16):
                    gn_stats(0, k)
                gn_channels(0)
                gn_scale(0)
                gn_bias(0)
                for k in range(8):
                    gn_apply(0, k)
                for j in range(NXC):
                    split_x(0, j)
                def turn(b, order):
                    for n, (kind, hp, i) in enumerate(order):
                        t = b * HP + hp
                        src = bank[:, bank_of(order, n), :]
                        if kind == "yh":
                            dve.wait_ge(y_st[i % YST], (t * (YH // YST) + (i // YST + 1)) * 32)
                            if hp == HP - 1 and i >= YST:
                                dve.wait_ge(sums, t * (2 * YH) + 6 + (i - YST + 1))
                            else:
                                dve.wait_ge(sums, (t * YH + i) * 2 + 4)
                        dve.wait_ge(hi_done, at(b, (kind, hp, i)) + 1)
                        if kind == "kv":
                            v = src.rearrange("p (j t n) -> p j t n", j=2, t=2)
                            dve.tensor_tensor(v_lo[:, hp % 2, 2 * i:2 * i + 2, 0:P], v[:, :, 1, :],
                                              v_hi[:, hp % 2, 2 * i:2 * i + 2, 0:P], ALU.subtract).then_inc(freed, 1)
                            if i % 8 == 7:
                                j = i // 8
                                dve.tensor_reduce(kmax_halves[:, j, :],
                                                  k_f[:, 16 * j:16 * j + 16, :].rearrange("p y c -> p c y"),
                                                  AX.X, ALU.max).then_inc(kmax_done, 1)
                            if i == KV - 1:
                                dve.wait_ge(kmax_done, t * 3 + 2)
                                dve.tensor_reduce(kmax[:, :], kmax_halves[:, :, :].rearrange("p y c -> p c y"),
                                                  AX.X, ALU.max).then_inc(kmax_done, 1)
                            if hp in (1, 2) and i >= 8 and order is not final_turn:
                                gn_stats(b + 1, (hp - 1) * 8 + (i - 8))
                            if hp == 3 and i >= 8 and order is not final_turn:
                                if i == 8:
                                    gn_bias(b + 1)
                                gn_apply(b + 1, i - 8)
                        elif kind == "q":
                            x0, h2 = (i // 2) * 16, i % 2
                            dve.tensor_tensor(q_lo[:, h2, x0:x0 + 16, :].rearrange("p x y -> p (x y)"), src,
                                              q_hi[:, h2, x0:x0 + 16, :].rearrange("p x y -> p (x y)"),
                                              ALU.subtract).then_inc(freed, 1)
                        elif kind == "sx":
                            for g in range(2):
                                s = slice(8 * i, 8 * i + 8)
                                o = dve.scalar_tensor_tensor(sx_lo[:, :, g, s],
                                                             src.rearrange("p (x h) -> p h x", x=8),
                                                             parity[:, g:g + 1], sx_hi[:, :, g, s],
                                                             ALU.mult, ALU.subtract)
                            o.then_inc(freed, 1)
                        else:
                            dve.tensor_copy(yst[:, i % YST, :], src).then_inc(freed, 1)
                            if hp == HP - 1:
                                if i == 0:
                                    dve.wait_ge(sums, t * (2 * YH) + 6)
                                else:
                                    dve.wait_ge(squares, i)
                                dve.tensor_tensor(acc[:, 1, :], acc[:, 1, :], ysq[:, i % YSQ, :],
                                                  ALU.add).then_inc(squares, 1)
                        for h, j in chain(order, n):
                            th = b * HP + h
                            if j == 2:
                                dve.wait_ge(small, th * 2 + 1)
                                dve.tensor_reduce(colmax[:, :], small_ps[:, 0:P], AX.X, ALU.max,
                                                  negate=True).then_inc(max_done, 1)
                                dve.wait_ge(max_done, th * 3 + 1)
                                dve.tensor_scalar(diag[:, :], ident[:, :], colmax[:, 0:1], None,
                                                  ALU.mult).then_inc(max_done, 1)
                            if j == 5:
                                dve.wait_ge(small, th * 2 + 2)
                                dve.tensor_copy(negmax[:, :], small_ps[:, P:2 * P]).then_inc(max_done, 1)
                            if 6 <= j < 10:
                                if j == 6:
                                    dve.wait_ge(max_done, th * 3 + 3)
                                kk = k_f[:, 8 * (j - 6):8 * (j - 6) + 8, :]
                                dve.tensor_tensor(kk, kk, negmax[:, :].unsqueeze(1).to_broadcast([P, 8, P]),
                                                  ALU.add).then_inc(shifted, 1)
                            if j == 9 and not (order is first_turn and h == 0):
                                context_out(dve, b * HP + (h - 1))
                            if 11 <= j < 13:
                                dve.wait_ge(p_hi_done, th * 4 + (j - 10))
                                s = slice(8 * (j - 11), 8 * (j - 11) + 8)
                                dve.tensor_tensor(p_lo[:, s, :], k_f[:, s, :], p_hi[:, s, :],
                                                  ALU.subtract).then_inc(p_lo_a, 1)
                            if (h, j) == (2, 1) and order is not final_turn:
                                gn_channels(b + 1)
                            if (h, j) == (2, 8) and order is not final_turn:
                                gn_scale(b + 1)
                        if kind == "yh" and hp == HP - 2 and i % 2 == 1 and order is not final_turn:
                            split_x(b + 1, i // 2)
                    if order is final_turn:
                        context_out(dve, b * HP + (HP - 1))

                turns(dve, turn)

            @block.gpsimd
            def _(pool):
                def split_x(nth, j):
                    pool.wait_ge(x_hi_b, nth * NXC + (j + 1))
                    s = slice(j * XC, j * XC + XC)
                    pool.tensor_tensor(x_lo[:, 1, s], x_f[:, 1, s], x_hi[:, 1, s], ALU.subtract).then_inc(x_lo_done, 1)

                def gn_power(nth):
                    pool.wait_ge(bn_done, nth * NBN + 26)
                    pool.tensor_tensor(rstd[:, :], rstd[:, :], minus_half[:, 0:CC], ALU.pow).then_inc(gn_root, 1)

                def take_last_sum(b, hp, i):
                    pool.wait_ge(freed, evacuated(b, ("yh", hp, i)))
                    pool.wait_ge(sums, (b * HP + hp) * (2 * YH) + 6 + i)
                    pool.tensor_tensor(acc[:, 0, :], acc[:, 0, :], yst[:, i % YST, :], ALU.add).then_inc(sums, 1)

                def take_sums(b, hp, i):
                    u = (b * HP + hp) * YH + i
                    pool.wait_ge(freed, evacuated(b, ("yh", hp, i)))
                    pool.wait_ge(sums, u * 2 + 5)
                    pool.tensor_tensor(acc[:, 0, :], acc[:, 0, :], yst[:, i % YST, :], ALU.add).then_inc(sums, 1)
                    pool.wait_ge(sums, u * 2 + 6)
                    pool.tensor_tensor(acc[:, 1, :], acc[:, 1, :], ysq[:, i % YSQ, :], ALU.add).then_inc(sums, 1)

                pool.memset(acc[:, :, :], 0.0).then_inc(sums, 6)
                gn_power(0)
                for j in range(XPOOL):
                    split_x(0, j)

                def split_p(t, j):
                    pool.wait_ge(p_hi_done, t * 4 + (j + 1))
                    s = slice(8 * j, 8 * j + 8)
                    pool.tensor_tensor(p_lo[:, s, :], k_f[:, s, :], p_hi[:, s, :], ALU.subtract).then_inc(p_lo_b, 1)

                def turn(b, order):
                    for n, (kind, hp, i) in enumerate(order):
                        if kind == "yh" and hp == HP - 1:
                            take_last_sum(b, hp, i)
                        elif kind == "yh":
                            take_sums(b, hp, i)
                        if (kind, hp, i) == ("yh", 1, YH - 1) and order is not final_turn:
                            gn_power(b + 1)
                        for h, j in chain(order, n):
                            if j == 15 and not (h == HP - 1 and order is not final_turn):
                                for quarter in (2, 3):
                                    split_p(b * HP + h, quarter)
                        if kind == "sx" and hp == HP - 1 and order is not final_turn:
                            if i < XPOOL:
                                split_x(b + 1, i)
                            elif i < XPOOL + 2:
                                split_p(b * HP + hp, i - XPOOL + 2)

                turns(pool, turn)

        SY, RO, PR = 8, 8, CC * 8
        SY_BEFORE = (0, 0, 0, 0, 1, 3, 5, 8)

        def turn2_of(first=False, final=False):
            order = [("sy", 0, i) for i in range(SY)] if first else []
            for hp in range(HP):
                done = 0
                for i in range(RO):
                    if hp == 0 and not first and i < RO // 2:
                        order += [("pr", -1, CC * (i + RO // 2) + m) for m in range(CC)]
                    if hp == HP - 1 and not final and i >= RO // 2:
                        order += [("pr", 0, CC * (i - RO // 2) + m) for m in range(CC)]
                    if not (final and hp == HP - 1):
                        order += [("sy", hp + 1, j) for j in range(done, SY_BEFORE[i])]
                        done = SY_BEFORE[i]
                    order.append(("ro", hp, i))
                    if final and hp == HP - 1 and i >= 2:
                        order += [("pr", 0, CC * (i - 2) + m) for m in range(CC)]
            return order + ([("pr", 0, u) for u in range(PR - 2 * CC, PR)] if final else [])

        first_turn2, loop_turn2, final_turn2 = turn2_of(first=True), turn2_of(), turn2_of(final=True)
        NF2 = len(loop_turn2)
        SHIFT2 = len(first_turn2) - NF2
        assert NF2 % BANKS == 0

        def at2(b, key):
            if isinstance(b, int) and b == 0:
                return first_turn2.index(key)
            kind, hp, i = key
            order = final_turn2 if isinstance(b, int) and b == NB - 1 else loop_turn2
            if kind == "sy" and hp == 0:
                return b * NF2 + (SHIFT2 + loop_turn2.index((kind, HP, i)) - NF2)
            return b * NF2 + (SHIFT2 + order.index(key))

        def evacuated2(b, key):
            return at2(b, key) + (BANKS + 1)

        def bank_of2(order, n):
            return (n if order is first_turn2 else n + SHIFT2) % BANKS

        def turns2(eng, turn):
            turn(0, first_turn2)
            with eng.Fori(1, NB - 1) as b:
                turn(b, loop_turn2)
            turn(NB - 1, final_turn2)

        YC = 4
        XY = H // YC
        XS = 4
        DVE_NORM = (2, 3)

        with ExitStack() as p2, nc.Block() as block:
            q2 = sb("q2", [P, 2, 2, 2, H, HALF], F16, p2)
            y_f = sb("y_f", [P, YC, XY, DK], F32, p2)
            yb_hi = sb("yb_hi", [P, H, 2, DK], F16, p2)
            yb_lo = sb("yb_lo", [P, H, 2, DK], F16, p2)
            sy_hi = sb("sy_hi", [P, 2, H, W], F16, p2)
            sy_lo = sb("sy_lo", [P, 2, H, W], F16, p2)
            o_hi = sb("o_hi", [P, HP, PIX], F16, p2)
            o_lo = sb("o_lo", [P, HP, PIX], F16, p2)
            wo_f = sb("wo_f2", [P, HP, C], F32, p2)
            wo_hi = sb("wo_hi", [P, HP, C], F16, p2)
            wo_lo = sb("wo_lo", [P, HP, C], F16, p2)
            c_f = sb("c_f", [P, DK], F32, p2)
            cb_hi = sb("cb_hi", [P, 2, 2, DK], F16, p2)
            cb_lo = sb("cb_lo", [P, 2, 2, DK], F16, p2)
            x_res = sb("x_res", [P, XS, BANK], F32, p2)
            bias = sb("bias", [P, CC], F32, p2)
            gam = sb("gam", [P, DK], F32, p2)
            bet = sb("bet", [P, DK], F32, p2)
            st = sb("st", [P, 2, DK], F32, p2)
            mean = sb("mean", [P, DK], F32, p2)
            var = sb("var", [P, DK], F32, p2)
            y_mul = sb("y_mul", [P, DK], F32, p2)
            y_add = sb("y_add", [P, DK], F32, p2)

            filled = sem("filled2", p2)
            hi_done = sem("hi_done2", p2)
            freed = sem("freed2", p2)
            const_in = sem("const_in", p2)
            stat = sem("stat", p2)
            stat_ps = sem("stat_ps", p2)
            root = sem("root", p2)
            init = sem("init2", p2)
            q_in = [sem(f"q_in{s}", p2) for s in range(2)]
            y_in = [sem(f"y_in{s}", p2) for s in range(YC)]
            c_in = sem("c_in", p2)
            x_in = [sem(f"xr_in{s}", p2) for s in range(XS)]
            y_norm = sem("y_norm", p2)
            y_norm_b = sem("y_norm_b", p2)
            yb_hi_done = sem("yb_hi_done", p2)
            yb_lo_done = sem("yb_lo_done", p2)
            cb_hi_done = sem("cb_hi_done", p2)
            cb_lo_done = sem("cb_lo_done", p2)
            out_st = [sem(f"out_st{s}", p2) for s in range(XS)]
            w_split = sem("w_split", p2)

            @block.sync
            def _(sp):
                def load_q(b, hp, c):
                    x0 = c * XY
                    for part in range(2):
                        sp.dma_start(q2[:, hp % 2, part, :, x0:x0 + XY, :].rearrange("p g x y -> p g (x y)"),
                                     q_dram[b * HP + hp].rearrange("h d l g n -> l (h d) g n")
                                     [part, :, :, x0 * HALF:(x0 + XY) * HALF]).then_inc(q_in[hp % 2], 16)

                def load_y(b, hp, c):
                    sp.dma_start(y_f[:, c, :, :].rearrange("p x e -> p (x e)"),
                                 y_dram[b * HP + hp].rearrange("g y h x e -> (g y h) (x e)")
                                 [:, c * XY * DK:(c + 1) * XY * DK]).then_inc(y_in[c], 16)

                def load_context(b, hp):
                    sp.dma_start(c_f[:, :], c_dram[b * HP + hp]).then_inc(c_in, 16)

                def load_residual(b, image, u):
                    m, nn = u % CC, u // CC
                    sp.wait_ge(out_st[u % XS], b * (PR // XS * 16) + (image * (PR // XS) + u // XS + 1) * 16)
                    sp.dma_start(x_res[:, u % XS, :], x_chunks[b + image, m][:, nn * BANK:(nn + 1) * BANK]
                                 ).then_inc(x_in[u % XS], 16)

                for s in range(XS):
                    sp.sem_inc(out_st[s], 16)
                for c in range(YC):
                    load_q(0, 0, c)
                    load_y(0, 0, c)
                load_context(0, 0)
                for c in range(YC):
                    load_q(0, 1, c)
                for c in range(YC):
                    sp.wait_ge(yb_lo_done, c + 1)
                    load_y(0, 1, c)
                sp.wait_ge(cb_lo_done, 1)
                load_context(0, 1)

                def turn(b, order):
                    for hp in range(HP):
                        more = order is not final_turn2 or hp + 2 < HP
                        for i in range(RO):
                            if hp == HP - 1 and i in (4, 5) and order is not final_turn2:
                                for m in range(CC):
                                    load_residual(b, 0, XS + CC * (i - 4) + m)
                            if hp == 0 and i < 2 and order is not first_turn2:
                                for m in range(CC):
                                    load_residual(b, -1, PR - XS + CC * i + m)
                            if i % 2 == 1 and more:
                                c = i // 2
                                sp.wait_ge(filled, at2(b, ("ro", hp, i)) + 1)
                                load_q(b, hp + 2, c)
                                sp.wait_ge(yb_lo_done, (b * HP + (hp + 1)) * YC + (c + 1))
                                load_y(b, hp + 2, c)
                            if i == 1 and more:
                                sp.wait_ge(cb_lo_done, b * HP + (hp + 2))
                                load_context(b, hp + 2)
                            if hp == HP - 2 and i == 5:
                                for u in range(XS):
                                    load_residual(b, 0, u)
                            if hp == HP - 1 and i == RO - 1 and order is not final_turn2:
                                for u in range(2 * XS, PR - XS):
                                    load_residual(b, 0, u)
                    if order is final_turn2:
                        for u in range(XS, PR):
                            load_residual(b, 0, u)

                turns2(sp, turn)
                for s in range(XS):
                    sp.wait_ge(out_st[s], 16 * (NB * PR // XS + 1))

            @block.tensor
            def _(pe):
                pe.wait_ge(stat, 1)
                pe.matmul(small_ps[:, 0:2 * DK], ones[:, :], st[:, :, :].rearrange("p s e -> p (s e)"),
                          start=True, stop=True).then_inc(stat_ps, 1)

                def turn(b, order):
                    for n, (kind, hp, i) in enumerate(order):
                        t = b * HP + hp
                        r = bank_of2(order, n)
                        pe.wait_ge(freed, at2(b, (kind, hp, i)) + 1)
                        if kind == "sy":
                            if i == 0:
                                pe.wait_ge(q_in[hp % 2], (b * 2 + (hp // 2 + 1)) * (32 * YC))
                            for j in range(8):
                                y = 8 * i + j
                                for k, (a, m) in enumerate(TERMS):
                                    mm = pe.matmul(bank[:, r, j * 64:j * 64 + 64],
                                                   (rc_hi, rc_lo)[a][:, 2 * (W - 1 - y):2 * (W - 1 - y) + P],
                                                   q2[:, hp % 2, m, y // HALF, :, y % HALF],
                                                   start=k == 0, stop=k == 2)
                        elif kind == "ro":
                            if i == 0:
                                pe.wait_ge(cb_lo_done, t + 1)
                                pe.wait_ge(freed, evacuated2(b, ("sy", hp, SY - 1)))
                            if i % 2 == 0:
                                pe.wait_ge(yb_lo_done, t * YC + (i // 2 + 1))
                            for k, (a, m) in enumerate(TERMS):
                                pe.matmul(bank[:, r, :], (cb_hi, cb_lo)[a][:, hp % 2, :, :].rearrange("p g e -> p (g e)"),
                                          q2[:, hp % 2, m, :, 8 * i:8 * i + 8, :].rearrange("p g x y -> p x g y"),
                                          start=k == 0, stop=False, skip_group_check=True)
                            for j in range(8):
                                xx = 8 * i + j
                                for k, (a, m) in enumerate(TERMS):
                                    mm = pe.matmul(bank[:, r, j * 64:j * 64 + 64],
                                                   (yb_hi, yb_lo)[a][:, xx, :, :].rearrange("p g e -> p (g e)"),
                                                   (sy_hi, sy_lo)[m][:, hp % 2, xx, :],
                                                   start=False, stop=(j == 7 and k == 2), skip_group_check=True)
                        else:
                            m, nn = i % CC, i // CC
                            if order is first_turn2 and i == 0:
                                pe.wait_ge(w_split, 3)
                            if hp == 0 and m == 0:
                                pe.wait_ge(freed, evacuated2(b, ("ro", HP - 1, nn)))
                            if hp == -1 and m == 0:
                                pe.wait_ge(freed, b * NF2 + (SHIFT2 + loop_turn2.index(("ro", HP - 1, nn)) - NF2 + BANKS + 1))
                            for h in range(HP):
                                for k, (a, mo) in enumerate(TERMS):
                                    mm = pe.matmul(bank[:, r, :], (wo_hi, wo_lo)[a][:, h, m * P:m * P + P],
                                                   (o_hi, o_lo)[mo][:, h, nn * BANK:(nn + 1) * BANK],
                                                   start=(h == 0 and k == 0), stop=(h == HP - 1 and k == 2))
                        mm.then_inc(filled, 1)

                turns2(pe, turn)

            @block.scalar
            def _(act):
                def split_context(t, hp):
                    act.wait_ge(c_in, t * 16 + 16)
                    for g in range(2):
                        s = slice(g * 64, g * 64 + 64)
                        o = act.activation(cb_hi[s, hp % 2, g, :], c_f[s, :], ACT.Copy)
                    o.then_inc(cb_hi_done, 1)

                def split_piece(t, c):
                    if isinstance(t, int) and t == 0 and c in DVE_NORM:
                        act.wait_ge(y_norm_b, 2 * (c - DVE_NORM[0]) + 2)
                    else:
                        act.wait_ge(y_norm, t * (2 * YC) + (2 * c + 2))
                    for g in range(2):
                        o = act.activation(yb_hi[:, c * XY:(c + 1) * XY, g, :], y_f[:, c, :, :], ACT.Copy,
                                           scale=parity[:, g:g + 1])
                    o.then_inc(yb_hi_done, 1)

                def store(b, image, u):
                    m, nn = u % CC, u // CC
                    act.wait_ge(freed, evacuated2(b, ("pr", image, u)))
                    act.dma_start(out_chunks[b + image, m][:, nn * BANK:(nn + 1) * BANK],
                                  x_res[:, u % XS, :]).then_inc(out_st[u % XS], 16)

                act.dma_start(gam[:, :], gamma.unsqueeze(0).to_broadcast([P, DK])).then_inc(const_in, 16)
                act.dma_start(bet[:, :], beta.unsqueeze(0).to_broadcast([P, DK])).then_inc(const_in, 16)
                act.dma_start(bias[:, :], b_out.rearrange("(c p) -> p c", p=P),
                              allow_slow_non_contiguous=True).then_inc(const_in, 16)
                act.dma_start(wo_f[:, :, :], w_out_t.rearrange("(a p) n -> p a n", p=P)).then_inc(const_in, 16)
                act.wait_ge(const_in, 64)
                act.wait_ge(init, 4)
                split_context(0, 0)

                LATER = 3

                def turn(b, order):
                    for n, (kind, hp, i) in enumerate(order):
                        t = b * HP + hp
                        src = bank[:, bank_of2(order, n), :]
                        if kind == "pr":
                            act.wait_ge(x_in[i % XS], b * (PR // XS * 16) + (hp * (PR // XS) + i // XS + 1) * 16)
                            act.activation(x_res[:, i % XS, :], x_res[:, i % XS, :], ACT.Identity,
                                           bias=bias[:, i % CC:i % CC + 1]).then_inc(hi_done, 1)
                        else:
                            act.wait_ge(filled, at2(b, (kind, hp, i)) + 1)
                        if kind == "sy":
                            act.activation(sy_hi[:, hp % 2, :, 8 * i:8 * i + 8],
                                           src.rearrange("p (y x) -> p x y", y=8), ACT.Copy).then_inc(hi_done, 1)
                            if hp == 0 and i % 2 == 1:
                                split_piece(0, i // 2)
                        elif kind == "ro":
                            act.activation(o_hi[:, hp, i * BANK:(i + 1) * BANK], src, ACT.Copy).then_inc(hi_done, 1)
                            if order is not final_turn2 or hp + 1 < HP:
                                if i == 0:
                                    split_context(t + 1, hp + 1)
                                if i % 2 == 1:
                                    split_piece(t + 1, i // 2)
                        if n >= LATER and order[n - LATER][0] == "pr":
                            store(b, order[n - LATER][1], order[n - LATER][2])
                    if order is final_turn2:
                        for u in range(PR - LATER, PR):
                            store(b, 0, u)

                turns2(act, turn)

            @block.vector
            def _(dve):
                for tile in (cb_hi, cb_lo):
                    dve.memset(tile[0:64, :, 1, :], 0.0).then_inc(init, 1)
                    dve.memset(tile[64:128, :, 0, :], 0.0).then_inc(init, 1)
                dve.sem_inc(freed, BANKS)
                dve.tensor_reduce(st[:, :, :], acc[:, :, :].rearrange("p s (g e) -> p s e g", e=DK), AX.X,
                                  ALU.add).then_inc(stat, 1)
                dve.wait_ge(const_in, 64)
                dve.wait_ge(stat_ps, 1)
                dve.tensor_scalar(mean[:, :], small_ps[:, 0:DK], 1.0 / N_BN, None, ALU.mult).then_inc(stat, 1)
                dve.tensor_scalar(var[:, :], small_ps[:, DK:2 * DK], 1.0 / N_BN, None, ALU.mult).then_inc(stat, 1)
                dve.wait_ge(stat, 3)
                dve.tensor_tensor(y_mul[:, :], mean[:, :], mean[:, :], ALU.mult).then_inc(stat, 1)
                dve.wait_ge(stat, 4)
                dve.tensor_tensor(var[:, :], var[:, :], y_mul[:, :], ALU.subtract).then_inc(stat, 1)
                dve.wait_ge(stat, 5)
                dve.tensor_scalar(var[:, :], var[:, :], factors[:, 1:2], factors[:, 1:2],
                                  ALU.mult, ALU.mult).then_inc(stat, 1)
                dve.wait_ge(stat, 6)
                dve.tensor_scalar(var[:, :], var[:, :], 0.0, BN_EPS, ALU.max, ALU.add).then_inc(stat, 1)
                dve.wait_ge(root, 1)
                dve.tensor_tensor(y_mul[:, :], var[:, :], gam[:, :], ALU.mult).then_inc(stat, 1)
                dve.wait_ge(stat, 8)
                dve.tensor_scalar(y_mul[:, :], y_mul[:, :], factors[:, 1:2], None, ALU.mult).then_inc(stat, 1)
                dve.wait_ge(stat, 9)
                dve.tensor_tensor(mean[:, :], mean[:, :], y_mul[:, :], ALU.mult).then_inc(stat, 1)
                dve.wait_ge(stat, 10)
                dve.tensor_tensor(y_add[:, :], bet[:, :], mean[:, :], ALU.subtract).then_inc(stat, 1)
                def split_context(t, hp):
                    dve.wait_ge(cb_hi_done, t + 1)
                    for g in range(2):
                        s = slice(g * 64, g * 64 + 64)
                        o = dve.tensor_tensor(cb_lo[s, hp % 2, g, :], c_f[s, :], cb_hi[s, hp % 2, g, :], ALU.subtract)
                    o.then_inc(cb_lo_done, 1)

                def normalise_first(c):
                    yy = y_f[:, c, :, :]
                    dve.wait_ge(stat, 11)
                    dve.wait_ge(y_in[c], 16)
                    dve.tensor_tensor(yy, yy, y_mul[:, :].unsqueeze(1).to_broadcast([P, XY, DK]),
                                      ALU.mult).then_inc(y_norm_b, 1)
                    dve.wait_ge(y_norm_b, 2 * (c - DVE_NORM[0]) + 1)
                    dve.tensor_tensor(yy, yy, y_add[:, :].unsqueeze(1).to_broadcast([P, XY, DK]),
                                      ALU.add).then_inc(y_norm_b, 1)

                def split_piece(t, c):
                    dve.wait_ge(yb_hi_done, t * YC + (c + 1))
                    for g in range(2):
                        s = slice(c * XY, (c + 1) * XY)
                        o = dve.scalar_tensor_tensor(yb_lo[:, s, g, :], y_f[:, c, :, :], parity[:, g:g + 1],
                                                     yb_hi[:, s, g, :], ALU.mult, ALU.subtract)
                    o.then_inc(yb_lo_done, 1)

                split_context(0, 0)

                def turn(b, order):
                    for n, (kind, hp, i) in enumerate(order):
                        t = b * HP + hp
                        dve.wait_ge(hi_done, at2(b, (kind, hp, i)) + 1)
                        src = bank[:, bank_of2(order, n), :]
                        if kind == "sy":
                            s = slice(8 * i, 8 * i + 8)
                            dve.tensor_tensor(sy_lo[:, hp % 2, :, s], src.rearrange("p (y x) -> p x y", y=8),
                                              sy_hi[:, hp % 2, :, s], ALU.subtract).then_inc(freed, 1)
                            if hp == 0 and i in (3, 5):
                                normalise_first((i + 1) // 2)
                            if hp == 0 and i % 2 == 1:
                                split_piece(0, i // 2)
                        elif kind == "ro":
                            s = slice(i * BANK, (i + 1) * BANK)
                            dve.tensor_tensor(o_lo[:, hp, s], src, o_hi[:, hp, s], ALU.subtract).then_inc(freed, 1)
                            if order is not final_turn2 or hp + 1 < HP:
                                if i == 0:
                                    split_context(t + 1, hp + 1)
                                if i % 2 == 1:
                                    split_piece(t + 1, i // 2)
                            if order is first_turn2 and hp == 0 and i == RO - 1:
                                dve.tensor_scalar(wo_f[:, :, :], wo_f[:, :, :], inv_all[:, 3:4], None,
                                                  ALU.mult).then_inc(w_split, 1)
                                dve.wait_ge(w_split, 1)
                                dve.tensor_copy(wo_hi[:, :, :], wo_f[:, :, :]).then_inc(w_split, 1)
                                dve.wait_ge(w_split, 2)
                                dve.tensor_tensor(wo_lo[:, :, :], wo_f[:, :, :], wo_hi[:, :, :],
                                                  ALU.subtract).then_inc(w_split, 1)
                        else:
                            dve.wait_ge(filled, at2(b, (kind, hp, i)) + 1)
                            dve.scalar_tensor_tensor(x_res[:, i % XS, :], src, factors[:, 2:3],
                                                     x_res[:, i % XS, :], ALU.mult, ALU.add).then_inc(freed, 1)

                turns2(dve, turn)

            @block.gpsimd
            def _(pool):
                pool.wait_ge(stat, 7)
                pool.tensor_tensor(var[:, :], var[:, :], minus_half[:, :], ALU.pow).then_inc(root, 1)
                pool.wait_ge(stat, 11)

                def normalise(t, pieces):
                    for c in pieces:
                        yy = y_f[:, c, :, :]
                        pool.wait_ge(y_in[c], t * 16 + 16)
                        pool.tensor_tensor(yy, yy, y_mul[:, :].unsqueeze(1).to_broadcast([P, XY, DK]),
                                           ALU.mult).then_inc(y_norm, 1)
                        pool.wait_ge(y_norm, t * (2 * YC) + (2 * c + 1))
                        pool.tensor_tensor(yy, yy, y_add[:, :].unsqueeze(1).to_broadcast([P, XY, DK]),
                                           ALU.add).then_inc(y_norm, 1)

                normalise(0, range(DVE_NORM[0]))
                pool.wait_ge(y_norm, 2 * DVE_NORM[0])
                pool.sem_inc(y_norm, 2 * len(DVE_NORM))
                with pool.Fori(1, NT) as t:
                    normalise(t, range(YC))


def kernel(x, L0_conv_w_qkv, L0_conv_w_out, L0_conv_b_out, L0_conv_rel_rows, L0_conv_rel_columns,
           L0_conv_bn_gamma, L0_conv_bn_beta):
    import numpy as np
    import concourse.bacc as bacc
    from concourse.bass_utils import run_bass_kernel_spmd

    nc = bacc.Bacc("TRN2", target_bir_lowering=False, num_devices=1)
    arrays = {
        "x": np.ascontiguousarray(x),
        "w_qkv_t": np.ascontiguousarray(np.asarray(L0_conv_w_qkv).T),
        "w_out_t": np.ascontiguousarray(np.asarray(L0_conv_w_out).T),
        "b_out": np.ascontiguousarray(L0_conv_b_out),
        "rel_rows_t": np.ascontiguousarray(np.asarray(L0_conv_rel_rows).T),
        "rel_cols_t": np.ascontiguousarray(np.asarray(L0_conv_rel_columns).T),
        "gamma": np.ascontiguousarray(L0_conv_bn_gamma),
        "beta": np.ascontiguousarray(L0_conv_bn_beta),
        "ident_in": np.eye(128, dtype=np.float32),
        "group_in": np.kron(np.eye(16, dtype=np.float32), np.full((8, 8), 0.125, np.float32)),
        "parity_in": np.eye(2, dtype=np.float32)[np.arange(128) % 2],
    }
    args = [nc.dram_tensor(n, a.shape, mybir.dt.from_np(a.dtype), kind="ExternalInput").ap()
            for n, a in arrays.items()]
    out = nc.dram_tensor("out", arrays["x"].shape, F32, kind="ExternalOutput").ap()
    attention_kernel(nc, *args, out)
    r = run_bass_kernel_spmd(nc, [arrays], core_ids=[0])
    return r.results[0]["out"]
```
